# Optimizing a Trainium2 kernel written in Bass

```python
import numpy as np
import jax
import jax.numpy as jnp

def _softmax(x, axis=-1):
    return jax.nn.softmax(x, axis=axis)

def _gelu(x):
    return jax.nn.gelu(x, approximate=True)

def _silu(x):
    return jax.nn.silu(x)

def _sigmoid(x):
    return jax.nn.sigmoid(x)

def _layernorm(x, axis=-1, eps=1e-05):
    m = jnp.mean(x, axis=axis, keepdims=True)
    v = jnp.var(x, axis=axis, keepdims=True)
    return (x - m) / jnp.sqrt(v + eps)

def _scatter_add(tgt, idx, src, axis=0):
    return tgt.at[idx].add(src)

def _segment_sum(src, seg, n):
    return jax.ops.segment_sum(src, seg, n)
kernel_name = 'mk_metaformer_d1_conv_nchw256_r4_f57372'

def setup_inputs(seed: int=0):
    np.random.seed(seed)
    _w = jnp.asarray

    def _rec_inputs():
        import jax
        import jax.numpy as jnp
        _gk = jax.random.key(seed)
        x = -7.109e-05 + 0.9999 * jax.random.normal(jax.random.fold_in(_gk, 1), (16, 64, 32, 32), jnp.float32)
        return x
    x = _rec_inputs()

    def _L0_conv_setup():
        import jax, jax.numpy as jnp
        import numpy as np
        B, C, H, W_ = (16, 64, 32, 32)
        key = jax.random.key(seed)
        k1, k2 = jax.random.split(key)
        x = jax.random.normal(k1, (B, C, H, W_), dtype=jnp.float32)
        Wm = jax.random.normal(k2, (C, C), dtype=jnp.float32) * (1.0 / np.sqrt(C))
        b = jnp.zeros((C,), dtype=jnp.float32)
        return {'x': x, 'W': Wm, 'b': b}
    _L0_conv_all = _L0_conv_setup()
    _L0_conv_in = {k: v for k, v in _L0_conv_all.items() if k in ('W', 'b')}
    del _L0_conv_all

    def _L0_ffn_setup():
        import math
        import jax, jax.numpy as jnp
        import numpy as np
        CAPACITY_FACTOR = 1.25
        key = jax.random.key(seed)
        ks = jax.random.split(key, 5)
        B, L, D, F, E = (8, 2048, 64, 256, 8)
        h = jax.random.normal(ks[0], (B, L, D), dtype=jnp.float32)
        gate_w = jax.random.normal(ks[1], (D, E), dtype=jnp.float32) * 0.02
        gate_b = jnp.zeros((E,), dtype=jnp.float32)
        w1 = jax.random.normal(ks[2], (E, D, F), dtype=jnp.float32) * (1.0 / math.sqrt(D))
        b1 = jnp.zeros((E, F), dtype=jnp.float32)
        w2 = jax.random.normal(ks[3], (E, F, D), dtype=jnp.float32) * (1.0 / math.sqrt(F))
        b2 = jnp.zeros((E, D), dtype=jnp.float32)
        return {'h': h, 'gate_w': gate_w, 'gate_b': gate_b, 'w1': w1, 'b1': b1, 'w2': w2, 'b2': b2}
    _L0_ffn_all = _L0_ffn_setup()
    _L0_ffn_in = {k: v for k, v in _L0_ffn_all.items() if k in ('gate_w', 'gate_b', 'w1', 'b1', 'w2', 'b2')}
    del _L0_ffn_all
    return {'x': x, 'L0_conv_W': _L0_conv_in['W'], 'L0_conv_b': _L0_conv_in['b'], 'L0_ffn_gate_w': _L0_ffn_in['gate_w'], 'L0_ffn_gate_b': _L0_ffn_in['gate_b'], 'L0_ffn_w1': _L0_ffn_in['w1'], 'L0_ffn_b1': _L0_ffn_in['b1'], 'L0_ffn_w2': _L0_ffn_in['w2'], 'L0_ffn_b2': _L0_ffn_in['b2']}

def reference(x, L0_conv_W, L0_conv_b, L0_ffn_gate_w, L0_ffn_gate_b, L0_ffn_w1, L0_ffn_b1, L0_ffn_w2, L0_ffn_b2):
    import jax
    import jax.numpy as jnp

    def _L0_conv_ref(x, W, b):
        import jax, jax.numpy as jnp
        import numpy as np
        B, C, H, W_ = (16, 64, 32, 32)
        cf = jnp.fft.fft2(x, axes=(-2, -1)).real.mean(axis=(-2, -1))
        cf = jax.nn.sigmoid(cf @ W.T + b)
        x_cft = x * cf[:, :, None, None]
        sf = jnp.fft.fft2(x.mean(axis=1, keepdims=True), axes=(-2, -1)).real.mean(axis=1)
        x_sft = x * sf[:, None, :, :]
        return x_cft + x_sft

    def _L0_ffn_ref(h, gate_w, gate_b, w1, b1, w2, b2):
        import math
        import jax, jax.numpy as jnp
        import numpy as np
        CAPACITY_FACTOR = 1.25
        B, L, D = h.shape
        E = gate_w.shape[1]
        T = B * L
        C = max(1, math.ceil(CAPACITY_FACTOR * T / E))
        x = h.reshape(T, D)
        logits = x @ gate_w + gate_b
        probs = jax.nn.softmax(logits, axis=-1)
        idx = jnp.argmax(probs, axis=-1)
        prb = jnp.take_along_axis(probs, idx[:, None], axis=1)[:, 0]
        one_hot = jax.nn.one_hot(idx, E, dtype=jnp.float32)
        pos = (jnp.cumsum(one_hot, axis=0) * one_hot).sum(-1).astype(jnp.int32) - 1
        kept = pos < C
        pos_safe = jnp.where(kept, pos, C)
        buf = jnp.zeros((E, C, D), dtype=h.dtype).at[idx, pos_safe].set(x, mode='drop')
        hmid = jax.nn.relu(jnp.einsum('ecd,edf->ecf', buf, w1) + b1[:, None, :])
        ybuf = jnp.einsum('ecf,efd->ecd', hmid, w2) + b2[:, None, :]
        pos_g = jnp.minimum(pos, C - 1)
        y_tok = ybuf[idx, pos_g] * (prb * kept)[:, None]
        y = y_tok.reshape(B, L, D)
        y = jnp.nan_to_num(y, nan=0.0, posinf=10000.0, neginf=-10000.0)
        return y

    def _gn(v, G=32, eps=1e-05):
        B_, C_, H_, W_ = v.shape
        g = v.reshape(B_, G, C_ // G, H_, W_)
        m = jnp.mean(g, axis=(2, 3, 4), keepdims=True)
        s = jnp.var(g, axis=(2, 3, 4), keepdims=True)
        return ((g - m) / jnp.sqrt(s + eps)).reshape(v.shape)

    def _ln_c(v, eps=1e-06):
        m = jnp.mean(v, axis=1, keepdims=True)
        s = jnp.var(v, axis=1, keepdims=True)
        return (v - m) / jnp.sqrt(s + eps)

    def _ln_t(v, eps=1e-05):
        m = jnp.mean(v, axis=-1, keepdims=True)
        s = jnp.var(v, axis=-1, keepdims=True)
        return (v - m) / jnp.sqrt(s + eps)

    def _to_tokens(v):
        B_, C_, H_, W_ = v.shape
        return v.reshape(B_, C_, H_ * W_).transpose(0, 2, 1)

    def _from_tokens(t, like):
        B_, C_, H_, W_ = like.shape
        return t.transpose(0, 2, 1).reshape(B_, C_, H_, W_)
    x = x + _L0_conv_ref(_ln_c(x), L0_conv_W, L0_conv_b)
    t = _to_tokens(x)
    t = t + _L0_ffn_ref(_ln_t(t), L0_ffn_gate_w, L0_ffn_gate_b, L0_ffn_w1, L0_ffn_b1, L0_ffn_w2, L0_ffn_b2)
    x = _from_tokens(t, x)
    return x

_drawn_inputs = setup_inputs


def setup_inputs(seed=0):
    import zlib

    import numpy as np

    out = dict(_drawn_inputs(seed))
    spreads = {'L0_conv_b': (0.0, 0.529),
     'L0_ffn_gate_b': (0.0, 0.1),
     'L0_ffn_b1': (0.0, 0.8),
     'L0_ffn_b2': (0.0, 0.8)}
    factors = {}
    for name, (base, spread) in spreads.items():
        noise = np.random.default_rng([zlib.crc32(name.encode()), seed]).standard_normal(out[name].shape)
        drawn = base * np.exp(spread * noise) if base else spread * noise
        out[name] = jnp.asarray(drawn.astype(out[name].dtype))
    for name, factor in factors.items():
        out[name] = (out[name] * factor).astype(out[name].dtype)
    return out
```

```python
import concourse.bass as bass
from concourse import mybir
from contextlib import ExitStack

NB, C, HW = 16, 64, 1024
P = 128
NG = NB // 2
TT = HW // P
S = 2 * TT
E, F = 8, 256
NTOK = NB * HW
CAP = -(-NTOK * 5 // (4 * E))
SLOTS = E * CAP
ROW = C + 2
ST = CAP // P
UT = 4
NU = ST // UT
YB = 5
SIDE = 32
RSQRT_SEED = float(0x5F3759DF)


class Group:

    def __init__(self, loop, offset):
        self.g = 2 * loop + offset
        self.u = offset % 2
        self.half = loop + offset // 2


def build(nc, x, conv_w, conv_b, gate_w, gate_b, w1, b1, w2, b2, const, dft, out):
    fp32, bf16, u32, i32 = mybir.dt.float32, mybir.dt.bfloat16, mybir.dt.uint32, mybir.dt.int32
    ALU, ACT, AX = mybir.AluOpType, mybir.ActivationFunctionType, mybir.AxisListType

    slot_rows = nc.dram_tensor("slot_rows", (SLOTS, ROW), fp32, kind="Internal").ap()
    token_out = nc.dram_tensor("token_out", (NTOK, C), fp32, kind="Internal").ap()
    x_rows = x.rearrange("b c h w -> (b c) (h w)")
    out_rows = out.rearrange("b c h w -> (b c) (h w)")

    with ExitStack() as ctx:
        def sb(name, shape, dt=fp32):
            return ctx.enter_context(nc.sbuf_tensor(name, shape, dt))

        def ps(name, shape):
            return ctx.enter_context(nc.psum_tensor(name, shape, fp32))

        def sem(name):
            return ctx.enter_context(nc.semaphore(name))

        kc = sb("kc", [P, const.shape[1]])
        at = 0
        views = []
        for width in (P, P, P, P, 2 * P, 4, P, P, S):
            views.append(kc[:, at:at + width])
            at += width
        ident, centre, before, ones, dft_rows, own_q, scan_keep, e_less_8, token_of = views
        dft_cols = sb("dft_cols", [S, 8, C])
        ones_row = ones[0:1, :]
        gw = sb("gw", [P, 2 * E])
        cgw = sb("cgw", [P, 2 * E])
        gb8 = sb("gb8", [P, E])
        gb = sb("gb", [P, 2, E, TT])
        cw = sb("cw", [C, C])
        cwT = sb("cwT", [C, C])
        cb = sb("cb", [1, P])
        b1r = sb("b1r", [2 * E, P])
        b1T = sb("b1T", [P, E, 2])
        b2b = sb("b2b", [P, E, C])
        w1s = [sb(f"w1s{i}", [P, F]) for i in range(2)]
        b1s = [sb(f"b1s{i}", [P, 2]) for i in range(2)]
        w2s = [sb(f"w2s{i}", [P, 2, C]) for i in range(2)]
        empty_row = sb("empty_row", [P, ST, ROW])
        zero_row = sb("zero_row", [P, S, C])

        x_in = [sb(f"x_in{i}", [P, HW]) for i in range(2)]
        sq1 = sb("sq1", [P, S, C])
        xn = sb("xn", [P, S, C])
        mix = sb("mix", [P, S, C])
        x1 = sb("x1", [P, S, C])
        x1_all = sb("x1_all", [P, NG, HW])
        x1T = sb("x1T", [P, HW])
        sq2 = sb("sq2", [P, S, C])
        vv = [sb(f"vv{i}", [P, S]) for i in range(2)]
        rstd = [sb(f"rstd{i}", [P, S]) for i in range(2)]
        nq = [sb(f"nq{i}", [P, S]) for i in range(2)]
        mean_n = sb("mean_n", [P, S])
        col = sb("col", [C, 2])
        colb = sb("colb", [C, 2, P])
        row_freq = sb("row_freq", [S, 2 * P, 4])
        cf_exp = sb("cf_exp", [P, P])
        cf_den = sb("cf_den", [P, P])
        cf = sb("cf", [P, P])
        sf_all = sb("sf_all", [P, 2, 4, TT])
        sf = sb("sf", [P, S])
        lg = sb("lg", [P, 2, E, TT])
        lgb = sb("lgb", [P, 2, E, TT])
        top = sb("top", [P, S])
        below = sb("below", [P, 2, E, TT])
        cand = sb("cand", [P, 2, E, TT])
        expo = sb("expo", [P, 2, E, TT])
        den = sb("den", [P, S])
        pick = sb("pick", [P, S])
        hot = sb("hot", [P, 2, E, TT])
        run = sb("run", [P, 2, E, TT])
        carry = sb("carry", [P, E])
        start = sb("start", [P, 2, E])
        place = sb("place", [P, 2, E, TT])
        own = sb("own", [P, 2, E, TT])
        rank = sb("rank", [P, S])
        slot_f = sb("slot_f", [P, S])
        over = sb("over", [P, S])
        token_f = sb("token_f", [P, S])
        rows = [sb(f"rows{i}", [P, S, ROW]) for i in range(2)]
        slots = [sb(f"slots{i}", [P, S], u32) for i in range(2)]

        slot_in = [sb(f"slot_in{i}", [P, ST, ROW]) for i in range(2)]
        packed = [sb(f"packed{i}", [P, ST, C]) for i in range(2)]
        xT = [sb(f"xT{i}", [P, 2 * P]) for i in range(2)]
        hid = [sb(f"hid{i}", [P, 2, 2, 2 * P]) for i in range(2)]
        y0 = sb("y0", [P, UT, C])
        bad = sb("bad", [P, UT, C])
        neg = sb("neg", [P, UT, C])
        pos = sb("pos", [P, UT, C])
        edge = sb("edge", [P, UT, C])
        wait_here = sb("wait_here", [P, 1])
        pool_zero = sb("pool_zero", [P, 1])
        pool_tick = sb("pool_tick", [P, 1])
        ys = [sb(f"ys{i}", [P, UT, C]) for i in range(YB)]

        y_in = [sb(f"y_in{i}", [P, 2, TT, C]) for i in range(2)]
        total = [sb(f"total{i}", [P, S, C]) for i in range(2)]
        o_sb = [sb(f"o_sb{i}", [P, HW]) for i in range(2)]

        psX = ps("psX", [P, HW])
        psC = ps("psC", [P, HW])
        psD = ps("psD", [P, HW])
        psT = ps("psT", [P, 512])
        psM = ps("psM", [P, 512])
        p_freq = psM[0:S, 0:2 * P]
        p_cf = psM[:, 0:P]
        p_col = psM[0:C, 256:258]
        p_sf = psM[:, 258:258 + C]
        p_base = psM[:, 322:322 + 2 * E]
        p_sum = psM[:, 338:338 + E]
        p_log = psM[:, 384:384 + P]

        const_in = sem("const_in")
        gw_zero = sem("gw_zero")
        zero_set = sem("zero_set")
        pool_ticked = sem("pool_ticked")
        weights_in = sem("weights_in")
        setup_mm = sem("setup_mm")
        setup_done = sem("setup_done")
        empty_set = sem("empty_set")
        slot_init = sem("slot_init")
        token_init = sem("token_init")
        x_loaded = [sem(f"x_loaded{i}") for i in range(2)]
        x_centred = sem("x_centred")
        x_turned = sem("x_turned")
        squared1 = sem("squared1")
        squared2 = sem("squared2")
        xn_done = sem("xn_done")
        mean_done = sem("mean_done")
        col_mm = sem("col_mm")
        col_done = sem("col_done")
        freq_mm = sem("freq_mm")
        freq_done = sem("freq_done")
        cf_mm = sem("cf_mm")
        cf_exp_done = sem("cf_exp_done")
        sf_mm = sem("sf_mm")
        sf_read = sem("sf_read")
        x1_done = sem("x1_done")
        x1_kept = sem("x1_kept")
        x1_turned = sem("x1_turned")
        x1T_done = sem("x1T_done")
        x1_centred = sem("x1_centred")
        logits_mm = sem("logits_mm")
        logits_read = sem("logits_read")
        below_done = sem("below_done")
        exp_done = sem("exp_done")
        numbered = sem("numbered")
        run_done = sem("run_done")
        base_mm = sem("base_mm")
        base_read = sem("base_read")
        rows_done = sem("rows_done")
        slots_done = sem("slots_done")
        rows_out = [sem(f"rows_out{i}") for i in range(2)]
        dve_step = sem("dve_step")
        slot_loaded = [sem(f"slot_loaded{i}") for i in range(2)]
        w_loaded = [sem(f"w_loaded{i}") for i in range(2)]
        packed_done = sem("packed_done")
        b1_set = sem("b1_set")
        slots_turned = sem("slots_turned")
        xT_done = sem("xT_done")
        hid_mm = sem("hid_mm")
        hid_done = sem("hid_done")
        y_mm = sem("y_mm")
        y_read = sem("y_read")
        y_done = sem("y_done")
        y_out = [sem(f"y_out{i}") for i in range(YB)]
        y_loaded = [sem(f"y_loaded{i}") for i in range(2)]
        total_done = sem("total_done")
        out_turned = sem("out_turned")
        out_copied = sem("out_copied")
        stored = [sem(f"stored{i}") for i in range(2)]

        N_CONST = 2 * 16
        N_WEIGHTS = 8 * 16
        N_SETUP = 3
        A_STEPS = 43
        DVE_SETUP = 6
        DVE_A_END = DVE_SETUP + NG * A_STEPS

        def wait_past(engine, semaphore, value):
            if not isinstance(value, int) or value > 0:
                engine.wait_ge(semaphore, value)

        def each_group(engine, body):
            for g in range(2):
                body(Group(0, g))
            with engine.Fori(1, NG // 2) as k:
                for o in range(2):
                    body(Group(k, o))

        block = ctx.enter_context(nc.Block())

        @block.sync
        def _(sp):
            sp.dma_start(kc[:], const).then_inc(const_in, 16)
            sp.dma_start(dft_cols[:], dft.rearrange("k (a n) -> k a n", a=8)).then_inc(const_in, 16)
            for g in range(2):
                sp.dma_start(x_in[g][:], x_rows[g * P:(g + 1) * P, :]).then_inc(x_loaded[g], 16)
            sp.dma_start(gb8[:], gate_b.partition_broadcast(P)).then_inc(weights_in, 16)
            sp.dma_start(cw[:], conv_w).then_inc(weights_in, 16)
            for h in range(2):
                sp.dma_start(cb[0:1, h * C:(h + 1) * C],
                             conv_b.rearrange("(a n) -> a n", a=1)).then_inc(weights_in, 16)
            sp.dma_start(b1r[:], b1.rearrange("e (a f) -> (e a) f", a=2)).then_inc(weights_in, 16)
            sp.dma_start(b2b[:], b2.partition_broadcast(P)).then_inc(weights_in, 16)
            sp.wait_ge(gw_zero, 1)
            for h in range(2):
                sp.dma_start(gw[h * C:(h + 1) * C, h * E:(h + 1) * E], gate_w).then_inc(weights_in, 16)
            sp.wait_ge(empty_set, 2)
            for e in range(E):
                sp.dma_start(slot_rows[e * CAP:(e + 1) * CAP, :].rearrange("(p j) c -> p j c", p=P),
                             empty_row[:]).then_inc(slot_init, 16)
            for g in range(NG):
                sp.dma_start(token_out[g * S * P:(g + 1) * S * P, :].rearrange("(p j) c -> p j c", p=P),
                             zero_row[:]).then_inc(token_init, 16)
            with sp.Fori(0, NG // 2 - 1) as k:
                for u in range(2):
                    sp.wait_ge(x_turned, 2 * k + u + 1)
                    sp.dma_start(x_in[u][:], x_rows[bass.ds((2 * k + u + 2) * P, P), :]).then_inc(x_loaded[u], 16)

            def load_expert(k, u):
                e = 2 * k + u
                sp.dma_start(slot_in[u][:], slot_rows[bass.ds(e * CAP, CAP), :]
                             .rearrange("(p j) c -> p j c", p=P)).then_inc(slot_loaded[u], 16)
                w1e = w1[bass.ds(e, 1), :, :].rearrange("a d f -> (a d) f")
                for h in range(2):
                    sp.dma_start(w1s[u][h * C:(h + 1) * C, :], w1e).then_inc(w_loaded[u], 16)
                sp.dma_start(w2s[u][:], w2[bass.ds(e, 1), :, :]
                             .rearrange("a (h f) c -> (a f) h c", h=2)).then_inc(w_loaded[u], 16)

            for u in range(2):
                sp.wait_ge(rows_out[u], NG // 2 * S * 16)
            for u in range(2):
                load_expert(0, u)
            with sp.Fori(0, E // 2 - 1) as k:
                for u in range(2):
                    sp.wait_ge(y_mm, (2 * k + u + 1) * NU)
                    for b in range(YB):
                        sp.wait_ge(y_out[b], (2 * k + u + 1) * UT * 16)
                    load_expert(k + 1, u)

            def load_y(g, u):
                sp.dma_start(y_in[u][:], token_out[bass.ds(g * S * P, S * P), :]
                             .rearrange("(h p t) c -> p h t c", h=2, p=P)).then_inc(y_loaded[u], 16)

            for b in range(YB):
                sp.wait_ge(y_out[b], E * UT * 16)
            for u in range(2):
                load_y(u, u)
            with sp.Fori(0, NG // 2 - 1) as k:
                for u in range(2):
                    sp.wait_ge(total_done, 2 * k + u + 1)
                    load_y(2 * k + u + 2, u)
            for u in range(2):
                sp.wait_ge(stored[u], NG // 2 * 16)

        @block.gpsimd
        def _(pool):

            pool.wait_ge(zero_set, 1)
            pool.wait_ge(slot_init, E * 16)

            def tick():
                nc.gpsimd.tensor_tensor(pool_tick[:], pool_zero[:], pool_zero[:], ALU.add).then_inc(pool_ticked, 1)

            def dispatch(G):
                wait_past(pool, pool_ticked, G.g)
                pool.wait_ge(slots_done, G.g + 1)
                pool.wait_ge(rows_done, G.g + 1)
                pool.wait_ge(numbered, G.g + 1)
                tick()
                for s in range(S):
                    pool.indirect_dma_start(
                        out=slot_rows, out_offset=bass.IndirectOffsetOnAxis(ap=slots[G.u][:, s:s + 1], axis=0),
                        in_=rows[G.u][:, s, :], in_offset=None,
                        bounds_check=SLOTS - 1, oob_is_err=False).then_inc(rows_out[G.u], 16)

            each_group(pool, dispatch)
            pool.wait_ge(token_init, NG * 16)
            with pool.Fori(0, E // 2) as k:
                for local in range(2 * NU):
                    u, j = local // NU, local % NU
                    pool.wait_ge(pool_ticked, 2 * NU * k + local + NG)
                    pool.wait_ge(y_done, 2 * NU * k + local + 1)
                    tick()
                    ids = slot_in[u][:].bitcast(u32)
                    for i in range(UT):
                        n = UT * j + i
                        pool.indirect_dma_start(
                            out=token_out, out_offset=bass.IndirectOffsetOnAxis(ap=ids[:, n, C + 1:C + 2], axis=0),
                            in_=ys[local % YB][:, i, :], in_offset=None,
                            bounds_check=NTOK - 1, oob_is_err=False).then_inc(y_out[local % YB], 16)

        @block.scalar
        def _(act):
            act.wait_ge(setup_mm, N_SETUP)
            nc.scalar.copy(cgw[:], psM[:, 0:2 * E]).then_inc(setup_done, 1)
            nc.scalar.copy(cwT[:], psM[0:C, 64:64 + C]).then_inc(setup_done, 1)
            nc.scalar.copy(b1T[:].rearrange("p e a -> p (e a)"), psM[:, 128:128 + 2 * E]).then_inc(setup_done, 1)

            def front(G):
                g = G.g
                act.wait_ge(x_centred, g + 1)
                nc.scalar.activation(sq1[:].rearrange("p s c -> p (s c)"), psC[:], ACT.Square).then_inc(squared1, 1)
                act.wait_ge(col_mm, g + 1)
                nc.scalar.copy(colb[:], p_col.unsqueeze(2).to_broadcast([C, 2, P])).then_inc(col_done, 1)
                act.wait_ge(freq_mm, g + 1)
                nc.scalar.copy(row_freq[:], p_freq.unsqueeze(2).to_broadcast([S, 2 * P, 4])).then_inc(freq_done, 1)
                act.wait_ge(cf_mm, g + 1)
                nc.scalar.activation(cf_exp[:], p_cf, ACT.Exp, scale=-1.0).then_inc(cf_exp_done, 1)

            def back(G):
                g, u = G.g, G.u
                for half in range(2):
                    act.wait_ge(x1_turned, 2 * g + half + 1)
                    nc.scalar.copy(x1T[:, 512 * half:512 * (half + 1)], psT[:]).then_inc(x1T_done, 1)
                nc.scalar.copy(x1_all[:, bass.ds(g, 1), :].rearrange("p a n -> p (a n)"),
                               x1[:].rearrange("p s c -> p (s c)")).then_inc(x1_kept, 1)
                act.wait_ge(x1_centred, g + 1)
                nc.scalar.activation(sq2[:].rearrange("p s c -> p (s c)"), psD[:], ACT.Square).then_inc(squared2, 1)
                act.wait_ge(below_done, g + 1)
                nc.scalar.activation(expo[:], below[:], ACT.Exp).then_inc(exp_done, 1)

            def a_group(G):
                front(G)
                back(G)

            each_group(act, a_group)

            def unit(k, local):
                n, e, w = 2 * NU * k + local, 2 * k + local // NU, local % 2
                act.wait_ge(hid_mm, n + 1)
                act.wait_ge(b1_set, e + 1)
                for half in range(2):
                    hidden = (psX, psC)[w][:].rearrange("p (a f n) -> p a f n", a=2, f=2)[:, :, half, :]
                    nc.scalar.activation(hid[w][:, half, :, :], hidden, ACT.Relu, bias=b1s[local // NU][:, half:half + 1]).then_inc(hid_done, 1)
                
            def turn(k, local):
                n, e, u, w = 2 * NU * k + local, 2 * k + local // NU, local // NU, local % 2
                if local % NU == 0:
                    act.wait_ge(slot_loaded[u], 16 * (k + 1))
                    wait_past(act, slots_turned, (e - 1) * NU)
                    nc.scalar.copy(packed[u][:], slot_in[u][:, :, 0:C]).then_inc(packed_done, 1)
                    nc.scalar.copy(b1s[u][:], b1T[:, bass.ds(e, 1), :].rearrange("p a b -> p (a b)")).then_inc(b1_set, 1)
                act.wait_ge(slots_turned, n + 1)
                nc.scalar.copy(xT[w][:], psT[:, 256 * w:256 * (w + 1)]).then_inc(xT_done, 1)

            turn(0, 0)
            turn(0, 1)

            def pair(k, last):
                for local in range(2 * NU):
                    unit(k, local)
                    if not last or local + 2 < 2 * NU:
                        turn(k + (local + 2) // (2 * NU), (local + 2) % (2 * NU))

            pair(0, False)
            with act.Fori(1, E // 2 - 1) as k:
                pair(k, False)
            pair(E // 2 - 1, True)

            def c_group(G):
                act.wait_ge(out_turned, G.g + 1)
                nc.scalar.copy(o_sb[G.u][:].rearrange("q (p t) -> q t p", t=TT),
                               (psX, psC)[G.u][:].rearrange("q (t p) -> q t p", t=TT)).then_inc(out_copied, 1)
                act.wait_ge(out_copied, G.g + 1)
                act.dma_start(out_rows[bass.ds(G.g * P, P), :], o_sb[G.u][:]).then_inc(stored[G.u], 16)

            for g in range(2):
                c_group(Group(0, g))
            with act.Fori(1, NG // 2) as k:
                for o in range(2):
                    act.wait_ge(stored[o], k * 16)
                    c_group(Group(k, o))

        @block.vector
        def _(dve):
            nc.vector.memset(gw[:], 0.0).then_inc(gw_zero, 1)
            nc.vector.memset(zero_row[:], 0.0).then_inc(empty_set, 1)
            nc.vector.memset(empty_row[:], 1.0).then_inc(empty_set, 1)
            nc.vector.memset(pool_zero[:], 0.0).then_inc(zero_set, 1)
            nc.vector.memset(carry[:], 0.0).then_inc(dve_step, 1)
            dve.wait_ge(weights_in, N_WEIGHTS)
            nc.vector.tensor_copy(gb[:], gb8[:].unsqueeze(1).unsqueeze(3).to_broadcast([P, 2, E, TT])).then_inc(dve_step, 1)
            dve.wait_ge(const_in, N_CONST)
            nc.vector.tensor_copy(token_f[:], token_of).then_inc(dve_step, 1)
            dve.wait_ge(dve_step, 3)

            class Steps:

                def __init__(self, base):
                    self.base, self.n = base, 0

                def done(self, instruction):
                    instruction.then_inc(dve_step, 1)
                    self.n += 1
                    return self.n

                def wait(self, n):
                    dve.wait_ge(dve_step, self.base + n)

            def inverse_root(st, i, sums, eps):
                v, y, q = vv[i], rstd[i], nq[i]
                st.wait(sums)
                st.wait(st.done(nc.vector.tensor_scalar(v[:], v[:], 1.0 / C, eps, ALU.mult, ALU.add)))
                st.wait(st.done(nc.vector.tensor_scalar(y[:].bitcast(i32), v[:].bitcast(i32), -0.5, RSQRT_SEED,
                                                        ALU.mult, ALU.add)))
                for _ in range(3):
                    st.wait(st.done(nc.vector.tensor_tensor(q[:], y[:], y[:], ALU.mult)))
                    st.wait(st.done(nc.vector.scalar_tensor_tensor(q[:], q[:], -0.5, v[:], ALU.mult, ALU.mult)))
                    st.wait(st.done(nc.vector.scalar_tensor_tensor(y[:], q[:], 1.5, y[:], ALU.add, ALU.mult)))

            def over_c(tile):
                return tile[:].unsqueeze(2).to_broadcast([P, S, C])

            def thc(tile):
                return tile.rearrange("p (t h) c -> p t h c", h=2)

            def ht_e(tile):
                return tile[:].rearrange("p h e t -> p h t e")

            def th(tile):
                return tile[:].rearrange("p (t h) -> p h t", h=2)

            def over_e(tile):
                return th(tile).unsqueeze(2).to_broadcast([P, 2, E, TT])

            def front(G, st):
                g = G.g
                dve.wait_ge(squared1, g + 1)
                v = st.done(nc.vector.tensor_reduce(vv[0][:], sq1[:], AX.X, ALU.add))
                inverse_root(st, 0, v, 1e-6)
                nc.vector.tensor_tensor(xn[:], psC[:].rearrange("p (s c) -> p s c", c=C), over_c(rstd[0]),
                                        ALU.mult).then_inc(xn_done, 1)
                dve.wait_ge(xn_done, g + 1)
                nc.vector.tensor_reduce(mean_n[:], xn[:], AX.X, ALU.add).then_inc(mean_done, 1)
                dve.wait_ge(cf_exp_done, g + 1)
                st.wait(st.done(nc.vector.tensor_scalar(cf_den[:], cf_exp[:], 1.0, None, ALU.add)))
                st.wait(st.done(nc.vector.reciprocal(cf[:], cf_den[:])))
                dve.wait_ge(sf_mm, g + 1)
                nc.vector.tensor_tensor(
                    sf_all[:], p_sf.rearrange("p (h q t) -> p h q t", h=2, q=4),
                    own_q.unsqueeze(1).unsqueeze(3).to_broadcast([P, 2, 4, TT]), ALU.mult).then_inc(sf_read, 1)
                dve.wait_ge(sf_read, g + 1)
                st.wait(st.done(nc.vector.tensor_reduce(th(sf), sf_all[:].rearrange("p h q t -> p h t q"),
                                                        AX.X, ALU.add)))
                st.wait(st.done(nc.vector.tensor_tensor(
                    thc(mix[:]), cf[:].rearrange("p (h c) -> p h c", h=2).unsqueeze(1).to_broadcast([P, TT, 2, C]),
                    thc(over_c(sf)), ALU.add)))
                st.wait(st.done(nc.vector.tensor_tensor(mix[:], mix[:], xn[:], ALU.mult)))
                dve.wait_ge(x_turned, g + 1)
                wait_past(dve, x1_kept, g)
                wait_past(dve, x1_turned, 2 * g)
                nc.vector.tensor_tensor(x1[:], mix[:], psX[:].rearrange("p (s c) -> p s c", c=C),
                                        ALU.add).then_inc(x1_done, 1)

            def back(G, st):
                g, u = G.g, G.u
                dve.wait_ge(squared2, g + 1)
                v = st.done(nc.vector.tensor_reduce(vv[1][:], sq2[:], AX.X, ALU.add))
                inverse_root(st, 1, v, 1e-5)
                wait_past(dve, rows_out[u], G.half * S * 16)
                nc.vector.tensor_tensor(rows[u][:, :, 0:C], psD[:].rearrange("p (s c) -> p s c", c=C),
                                        over_c(rstd[1]), ALU.mult).then_inc(rows_done, 1)
                nc.vector.tensor_copy(rows[u][:].bitcast(u32)[:, :, C + 1], token_f[:]).then_inc(numbered, 1)
                dve.wait_ge(numbered, g + 1)
                numbers = st.done(nc.vector.tensor_scalar(token_f[:], token_f[:], float(S * P), None, ALU.add))
                dve.wait_ge(logits_mm, g + 1)
                nc.vector.tensor_tensor(
                    lg[:].rearrange("p h e t -> p t h e"), p_log.rearrange("p (t h e) -> p t h e", t=TT, h=2),
                    rstd[1][:].rearrange("p (t h) -> p t h", h=2).unsqueeze(3).to_broadcast([P, TT, 2, E]),
                    ALU.mult).then_inc(logits_read, 1)
                dve.wait_ge(logits_read, g + 1)
                st.wait(st.done(nc.vector.tensor_tensor(lgb[:], lg[:], gb[:], ALU.add)))
                st.wait(st.done(nc.vector.tensor_reduce(th(top), ht_e(lgb), AX.X, ALU.max)))
                nc.vector.tensor_tensor(below[:], lgb[:], over_e(top), ALU.subtract).then_inc(below_done, 1)
                dve.wait_ge(below_done, g + 1)
                st.wait(st.done(nc.vector.scalar_tensor_tensor(
                    cand[:].rearrange("p h e t -> p (h e t)"), below[:].rearrange("p h e t -> p (h e t)"), 0.0,
                    e_less_8, ALU.is_equal, ALU.mult)))
                st.wait(st.done(nc.vector.tensor_reduce(th(pick), ht_e(cand), AX.X, ALU.min)))
                hot_n = st.done(nc.vector.tensor_tensor(hot[:], cand[:], over_e(pick), ALU.is_equal))
                st.wait(hot_n)
                nc.vector.tensor_tensor_scan(run[:].rearrange("p h e t -> p (h e t)"), scan_keep,
                                             hot[:].rearrange("p h e t -> p (h e t)"), 0.0,
                                             ALU.mult, ALU.add).then_inc(run_done, 1)
                dve.wait_ge(exp_done, g + 1)
                st.wait(st.done(nc.vector.tensor_reduce(th(den), ht_e(expo), AX.X, ALU.add)))
                prob = st.done(nc.vector.reciprocal(rows[u][:, :, C], den[:]))
                dve.wait_ge(base_mm, g + 1)
                st.wait(st.done(nc.vector.tensor_tensor(
                    start[:], p_base.rearrange("p (h e) -> p h e", h=2),
                    carry[:].unsqueeze(1).to_broadcast([P, 2, E]), ALU.add)))
                nc.vector.tensor_tensor(carry[:], carry[:], p_sum, ALU.add).then_inc(base_read, 1)
                st.wait(st.done(nc.vector.tensor_tensor(
                    place[:], run[:], start[:].unsqueeze(3).to_broadcast([P, 2, E, TT]), ALU.add)))
                st.wait(st.done(nc.vector.tensor_tensor(own[:], place[:], hot[:], ALU.mult)))
                st.wait(st.done(nc.vector.tensor_reduce(th(rank), ht_e(own), AX.X, ALU.add)))
                st.done(nc.vector.scalar_tensor_tensor(slot_f[:], pick[:], float(CAP), rank[:], ALU.mult, ALU.add))
                st.wait(st.done(nc.vector.tensor_scalar(over[:], rank[:], float(CAP), float(1 << 20),
                                                        ALU.is_gt, ALU.mult)))
                st.wait(prob)
                st.wait(numbers)
                nc.vector.scalar_tensor_tensor(slots[u][:], slot_f[:], float(E * CAP - 1), over[:], ALU.add,
                                               ALU.add).then_inc(slots_done, 1)
                dve.wait_ge(slots_done, g + 1)
                dve.wait_ge(base_read, g + 1)

            def a_group(G):
                st = Steps(3 + A_STEPS * G.g)
                front(G, st)
                back(G, st)
                assert st.n == A_STEPS, st.n

            each_group(dve, a_group)

            def unit(k, local):
                n, e, u, j, w, b = 2 * NU * k + local, 2 * k + local // NU, local // NU, local % NU, local % 2, local % YB
                y = ys[b]
                st = Steps(3 + A_STEPS * NG + Y_STEPS * n)
                dve.wait_ge(y_mm, n + 1)
                nc.vector.tensor_tensor(y0[:], psD[:, 512 * w:512 * w + UT * C].rearrange("p (i c) -> p i c", c=C),
                                        b2b[:, bass.ds(e, 1), :].to_broadcast([P, UT, C]),
                                        ALU.add).then_inc(y_read, 1)
                dve.wait_ge(y_read, n + 1)
                wait_past(dve, y_out[b], (2 * k + u) * UT * 16)
                st.wait(st.done(nc.vector.tensor_tensor(
                    y[:], y0[:], slot_in[u][:, UT * j:UT * (j + 1), C:C + 1].to_broadcast([P, UT, C]), ALU.mult)))
                st.done(nc.vector.tensor_scalar(bad[:], y[:], 0.0, 0.0, ALU.mult, ALU.not_equal))
                st.done(nc.vector.tensor_scalar(neg[:], y[:], 0.0, -1e4, ALU.is_lt, ALU.mult))
                st.wait(st.done(nc.vector.tensor_scalar(pos[:], y[:], 0.0, 1e4, ALU.is_gt, ALU.mult)))
                edges = st.done(nc.vector.tensor_tensor(edge[:], neg[:], pos[:], ALU.add))
                st.wait(edges)
                nc.vector.memset(wait_here[:], 0.0)
                flat = "p i c -> p (i c)"
                nc.vector.copy_predicated(y[:].rearrange(flat), bad[:].bitcast(u32).rearrange(flat),
                                          edge[:].rearrange(flat)).then_inc(y_done, 1)
                dve.wait_ge(y_done, n + 1)

            Y_STEPS = 5
            for local in range(2 * NU):
                unit(0, local)
            with dve.Fori(1, E // 2) as k:
                for local in range(2 * NU):
                    unit(k, local)

            def c_group(G):
                dve.wait_ge(y_loaded[G.u], 16 * (G.half + 1))
                wait_past(dve, out_turned, G.g - 1)
                nc.vector.tensor_tensor(
                    total[G.u][:].rearrange("p (t h) c -> p h t c", h=2),
                    x1_all[:, bass.ds(G.g, 1), :].rearrange("p a (t h c) -> p (a h) t c", t=TT, h=2),
                    y_in[G.u][:], ALU.add).then_inc(total_done, 1)

            for g in range(2):
                dve.wait_ge(y_loaded[g], 16)
                nc.vector.tensor_tensor(
                    total[g][:].rearrange("p (t h) c -> p h t c", h=2),
                    x1_all[:, g, :].rearrange("p (t h c) -> p h t c", t=TT, h=2),
                    y_in[g][:], ALU.add).then_inc(total_done, 1)
            with dve.Fori(1, NG // 2) as k:
                for o in range(2):
                    c_group(Group(k, o))

        @block.tensor
        def _(pe):
            pe.wait_ge(const_in, N_CONST)
            pe.wait_ge(weights_in, N_WEIGHTS)
            nc.tensor.matmul(psM[:, 0:2 * E], centre, gw[:], start=True, stop=True).then_inc(setup_mm, 1)
            nc.tensor.transpose(psM[0:C, 64:64 + C], cw[:], ident[0:C, 0:C]).then_inc(setup_mm, 1)
            nc.tensor.transpose(psM[:, 128:128 + 2 * E], b1r[:], ident[0:2 * E, 0:2 * E]).then_inc(setup_mm, 1)
            pe.wait_ge(setup_done, N_SETUP)

            def front(G):
                g, u = G.g, G.u
                xv = x_in[u][:].rearrange("q (p t) -> q t p", t=TT)
                pe.wait_ge(x_loaded[u], 16 * (G.half + 1))
                wait_past(pe, xn_done, g)
                for t in range(TT):
                    last = nc.tensor.matmul(psC[:, t * P:(t + 1) * P], xv[:, t, :], centre, start=True, stop=True)
                last.then_inc(x_centred, 1)
                wait_past(pe, x1_done, g)
                for t in range(TT):
                    last = nc.tensor.transpose(psX[:, t * P:(t + 1) * P], xv[:, t, :], ident)
                last.then_inc(x_turned, 1)
                pe.wait_ge(xn_done, g + 1)
                wait_past(pe, base_read, g)
                for h in range(2):
                    last = nc.tensor.matmul(p_col[:, h:h + 1], xn[0:1, h, :], ones[0:1, 0:1], start=True, stop=True)
                last.then_inc(col_mm, 1)
                pe.wait_ge(mean_done, g + 1)
                pe.wait_ge(col_done, g + 1)
                nc.tensor.matmul(p_freq, mean_n[:], dft_rows, start=True, stop=True).then_inc(freq_mm, 1)
                pe.wait_ge(freq_done, g + 1)
                for h in range(2):
                    o = p_cf[:, h * C:(h + 1) * C]
                    nc.tensor.matmul(o, colb[:, h, :], cwT[:], start=True, stop=False)
                    last = nc.tensor.matmul(o, ones_row, cb[0:1, h * C:(h + 1) * C], start=False, stop=True)
                last.then_inc(cf_mm, 1)
                pe.wait_ge(cf_exp_done, g + 1)
                for a in range(8):
                    last = nc.tensor.matmul(p_sf, row_freq[:, a * 32:(a + 1) * 32, :].rearrange("k r q -> k (r q)"),
                                            dft_cols[:, a, :], start=(a == 0), stop=(a == 7))
                last.then_inc(sf_mm, 1)

            def back(G):
                g = G.g
                pe.wait_ge(x1_done, g + 1)
                for half in range(2):
                    wait_past(pe, x1T_done, 2 * g + half)
                    for i in range(TT // 2):
                        t = half * TT // 2 + i
                        last = nc.tensor.transpose(psT[:, i * P:(i + 1) * P],
                                                   x1[:, 2 * t:2 * t + 2, :].rearrange("p s c -> p (s c)"), ident)
                    last.then_inc(x1_turned, 1)
                pe.wait_ge(x1T_done, 2 * g + 2)
                wait_past(pe, rows_done, g)
                for t in range(TT):
                    last = nc.tensor.matmul(psD[:, t * P:(t + 1) * P], x1T[:, t * P:(t + 1) * P], centre,
                                            start=True, stop=True)
                last.then_inc(x1_centred, 1)
                pe.wait_ge(sf_read, g + 1)
                for t in range(TT):
                    last = nc.tensor.matmul(p_log[:, t * 2 * E:(t + 1) * 2 * E], x1T[:, t * P:(t + 1) * P], cgw[:],
                                            start=True, stop=True)
                last.then_inc(logits_mm, 1)
                pe.wait_ge(run_done, g + 1)
                pe.wait_ge(logits_read, g + 1)
                counts = run[:].rearrange("p h e t -> p (h e) t")[:, :, TT - 1]
                nc.tensor.matmul(p_base[:, 0:E], before, counts[:, 0:E], start=True, stop=True)
                nc.tensor.matmul(p_base[:, E:], before, counts[:, E:], start=True, stop=False)
                nc.tensor.matmul(p_base[:, E:], ones, counts[:, 0:E], start=False, stop=True)
                nc.tensor.matmul(p_sum, ones, counts[:, 0:E], start=True, stop=False)
                nc.tensor.matmul(p_sum, ones, counts[:, E:], start=False, stop=True).then_inc(base_mm, 1)

            def a_group(G):
                front(G)
                back(G)

            each_group(pe, a_group)

            def turn(k, local):
                n, u, j, w = 2 * NU * k + local, local // NU, local % NU, local % 2
                if j == 0:
                    pe.wait_ge(packed_done, 2 * k + u + 1)
                wait_past(pe, xT_done, n)
                for i in range(2):
                    s = UT * j + 2 * i
                    last = nc.tensor.transpose(
                        psT[:, 256 * w + P * i:256 * w + P * (i + 1)], packed[u][:, s:s + 2, :].rearrange("p s c -> p (s c)"), ident)
                last.then_inc(slots_turned, 1)

            def up(k, local):
                n, u, j, w = 2 * NU * k + local, local // NU, local % NU, local % 2
                if j == 0:
                    pe.wait_ge(w_loaded[u], 48 * (k + 1))
                pe.wait_ge(xT_done, n + 1)
                for half in range(2):
                    for a in range(2):
                        last = nc.tensor.matmul(
                            (psX, psC)[w][:, 512 * a + 256 * half:512 * a + 256 * (half + 1)],
                            w1s[u][C * a:C * (a + 1), P * half:P * (half + 1)], xT[w][C * a:C * (a + 1), :],
                            start=True, stop=True)
                last.then_inc(hid_mm, 1)

            def down(k, local):
                n, u, j, w = 2 * NU * k + local, local // NU, local % NU, local % 2
                pe.wait_ge(hid_done, 2 * n + 2)
                wait_past(pe, y_read, n - 1)
                for i in range(2):
                    for a in range(2):
                        o = psD[:, 512 * w + C * (2 * i + a):512 * w + C * (2 * i + a + 1)]
                        for half in range(2):
                            last = nc.tensor.matmul(o, hid[w][:, half, a, P * i:P * (i + 1)], w2s[u][:, half, :],
                                                    start=(half == 0), stop=(half == 1))
                last.then_inc(y_mm, 1)

            def pair(k, last):
                def there(local):
                    return (k + local // (2 * NU), local % (2 * NU))
                for local in range(2 * NU):
                    if not last or local + 1 < 2 * NU:
                        up(*there(local + 1))
                    if not last or local + 2 < 2 * NU:
                        turn(*there(local + 2))
                    down(k, local)

            turn(0, 0)
            turn(0, 1)
            up(0, 0)
            pair(0, False)
            with pe.Fori(1, E // 2 - 1) as k:
                pair(k, False)
            pair(E // 2 - 1, True)

            def c_group(G):
                pe.wait_ge(total_done, G.g + 1)
                for t in range(TT):
                    last = nc.tensor.transpose((psX, psC)[G.u][:, t * P:(t + 1) * P],
                                               total[G.u][:, 2 * t:2 * t + 2, :].rearrange("p s c -> p (s c)"), ident)
                last.then_inc(out_turned, 1)

            for g in range(2):
                c_group(Group(0, g))
            with pe.Fori(1, NG // 2) as k:
                for o in range(2):
                    pe.wait_ge(out_copied, 2 * k + o - 1)
                    c_group(Group(k, o))


_INS = ["x", "L0_conv_W", "L0_conv_b", "L0_ffn_gate_w", "L0_ffn_gate_b", "L0_ffn_w1", "L0_ffn_b1", "L0_ffn_w2",
        "L0_ffn_b2"]


def constants():
    import numpy as np

    p = np.arange(P)
    ident = np.eye(P)
    same_half = (p[:, None] // C == p[None, :] // C)
    centre = ident - same_half / C
    before = (p[:, None] < p[None, :]).astype(float)
    ones = np.ones((P, P))
    i, q = p // 4, p % 4
    turns = 2 * np.pi / SIDE
    u = np.arange(SIDE)
    rows = np.zeros((P, 2, 4, SIDE))
    for r in range(4):
        angle = turns * np.outer(i, u)
        rows[:, 0, r, :] = np.where(q[:, None] == r, np.cos(angle), 0) / C
        rows[:, 1, r, :] = np.where(q[:, None] == r, np.sin(angle), 0) / C
    own_q = (q[:, None] == np.arange(4)[None, :]).astype(float)
    keep = np.broadcast_to(np.arange(TT) != 0, (2 * E, TT)).reshape(1, -1).repeat(P, 0).astype(float)
    e_less_8 = np.broadcast_to((np.arange(E) - E)[None, :, None], (2, E, TT)).reshape(1, -1).repeat(P, 0)
    t, h = np.arange(S) // 2, np.arange(S) % 2
    token = TT * p[:, None] + t[None, :] + HW * h[None, :]
    const = np.concatenate([ident, centre, before, ones, rows.reshape(P, -1), own_q, keep, e_less_8, token], 1)
    cols = np.zeros((S, 2, 4, 2, SIDE))
    for s in range(S):
        for r in range(4):
            angle = turns * (8 * r + t[s]) * u
            cols[s, 0, r, h[s], :] = np.cos(angle)
            cols[s, 1, r, h[s], :] = -np.sin(angle)
    return const.astype(np.float32), cols.reshape(S, -1).astype(np.float32)


def kernel(**inputs):
    import numpy as _np
    import concourse.bacc as _bacc
    from concourse import mybir as _mybir
    from concourse.bass_utils import run_bass_kernel_spmd as _run

    nc = _bacc.Bacc("TRN2", target_bir_lowering=False, num_devices=1)
    arrays, args = {}, []
    const, dft = constants()
    for name, a in [(n, inputs[n]) for n in _INS] + [("const", const), ("dft", dft)]:
        a = _np.ascontiguousarray(a)
        arrays[f"in_{name}_dram"] = a
        args.append(nc.dram_tensor(f"in_{name}_dram", a.shape, _mybir.dt.from_np(a.dtype), kind="ExternalInput").ap())
    args.append(nc.dram_tensor("out_dram", (NB, C, 32, 32), _mybir.dt.float32, kind="ExternalOutput").ap())
    build(nc, *args)
    r = _run(nc, [arrays], core_ids=[0])
    return r.results[0]["out_dram"]
```

```python
import concourse.bass as bass
from concourse import mybir
from contextlib import ExitStack

NB, C, HW = 16, 64, 1024
P = 128
NG = NB // 2
TT = HW // P
S = 2 * TT
E, F = 8, 256
NTOK = NB * HW
CAP = -(-NTOK * 5 // (4 * E))
SLOTS = E * CAP
ROW = C + 2
ST = CAP // P
UT = 4
NU = ST // UT
YB = 5
W1P = 3 * F
WP = W1P + 2 * 3 * C
SIDE = 32
RSQRT_SEED = float(0x5F3759DF)


class Group:

    def __init__(self, loop, offset):
        self.g = 2 * loop + offset
        self.u = offset % 2
        self.half = loop + offset // 2


class Turn:

    def __init__(self, loop, offset, front=True, back=True, ahead=True):
        self.i = 2 * loop + offset
        self.front = Group(loop, offset) if front else None
        self.back = Group(loop, offset - 1) if back else None
        self.ahead = Group(loop, offset + 1) if ahead else None


def unit_at(k, local):
    k, local = k + local // (2 * NU), local % (2 * NU)
    return k, local, 2 * NU * k + local, 2 * k + local // NU, local // NU, local % NU, local % 2


def build(nc, x, conv_w, conv_b, gate_w, gate_b, w1, b1, w2, b2, const, dft, out):
    fp32, bf16, u32, i32 = mybir.dt.float32, mybir.dt.bfloat16, mybir.dt.uint32, mybir.dt.int32
    ALU, ACT, AX = mybir.AluOpType, mybir.ActivationFunctionType, mybir.AxisListType

    slot_rows = nc.dram_tensor("slot_rows", (SLOTS, ROW), fp32, kind="Internal").ap()
    token_out = nc.dram_tensor("token_out", (NTOK, C), fp32, kind="Internal").ap()
    w_parts = nc.dram_tensor("w_parts", (E, P, WP), bf16, kind="Internal").ap()
    b_parts = nc.dram_tensor("b_parts", (3, E, F + C), bf16, kind="Internal").ap()
    x_rows = x.rearrange("b c h w -> (b c) (h w)")
    out_rows = out.rearrange("b c h w -> (b c) (h w)")

    with ExitStack() as ctx:
        def sb(name, shape, dt=fp32):
            return ctx.enter_context(nc.sbuf_tensor(name, shape, dt))

        def ps(name, shape):
            return ctx.enter_context(nc.psum_tensor(name, shape, fp32))

        def sem(name):
            return ctx.enter_context(nc.semaphore(name))

        kc = sb("kc", [P, const.shape[1]])
        at = 0
        views = []
        for width in (P, P, P, P, 2 * P, 4, P, P, S):
            views.append(kc[:, at:at + width])
            at += width
        ident, centre, before, ones, dft_rows, own_q, scan_keep, e_less_8, token_of = views
        dft_cols = sb("dft_cols", [S, 8, C])
        ones_row = ones[0:1, :]
        gw = sb("gw", [P, 2 * E])
        cgw = sb("cgw", [P, 2 * E])
        gb8 = sb("gb8", [P, E])
        gb = sb("gb", [P, 2, E, TT])
        cw = sb("cw", [C, C])
        cwT = sb("cwT", [C, C])
        cb = sb("cb", [1, C])
        ncb = sb("ncb", [C, 1])
        w1_all = sb("w1_all", [P, E, F])
        w2_all = sb("w2_all", [P, E, 2, C])
        bias_all = sb("bias_all", [E, F + C])
        wp_all = sb("wp_all", [P, E, WP], bf16)
        bp_all = sb("bp_all", [E, 3, F + C], bf16)
        wp = [sb(f"wp{i}", [P, WP], bf16) for i in range(2)]
        bp = [sb(f"bp{i}", [3, F + C], bf16) for i in range(2)]
        ones3 = sb("ones3", [3, 4 * P], bf16)
        ident_b = sb("ident_b", [P, P], bf16)
        empty_row = sb("empty_row", [P, ST, ROW])
        zero_row = sb("zero_row", [P, S, C])

        x_in = [sb(f"x_in{i}", [P, HW]) for i in range(2)]
        sq1 = sb("sq1", [P, S, C])
        xn = sb("xn", [P, S, C])
        mix = sb("mix", [P, S, C])
        x1 = sb("x1", [P, S, C])
        x1_all = sb("x1_all", [P, NG, HW])
        x1T = sb("x1T", [P, HW])
        sq2 = sb("sq2", [P, S, C])
        vv = sb("vv", [P, 2, S])
        rstd = sb("rstd", [P, 2, S])
        nq = sb("nq", [P, 2, S])
        mean_n = sb("mean_n", [P, S])
        col = sb("col", [C, 2])
        colb = sb("colb", [C, 2, P])
        row_freq = sb("row_freq", [S, 2 * P, 4])
        cf_exp = sb("cf_exp", [C, 2])
        cf_den = sb("cf_den", [C, 2])
        cf_col = sb("cf_col", [C, 2])
        sf_all = sb("sf_all", [P, 2, 4, TT])
        sf = sb("sf", [P, S])
        lg = sb("lg", [P, 2, E, TT])
        lgb = sb("lgb", [P, 2, E, TT])
        top = sb("top", [P, S])
        below = sb("below", [P, 2, E, TT])
        cand = sb("cand", [P, 2, E, TT])
        expo = sb("expo", [P, 2, E, TT])
        den = sb("den", [P, S])
        pick = sb("pick", [P, S])
        hot = sb("hot", [P, 2, E, TT])
        run = sb("run", [P, 2, E, TT])
        carry = sb("carry", [P, E])
        start = sb("start", [P, 2, E])
        place = sb("place", [P, 2, E, TT])
        own = sb("own", [P, 2, E, TT])
        rank = sb("rank", [P, S])
        slot_f = sb("slot_f", [P, S])
        over = sb("over", [P, S])
        token_f = sb("token_f", [P, S])
        rows = [sb(f"rows{i}", [P, S, ROW]) for i in range(2)]
        slots = [sb(f"slots{i}", [P, S], u32) for i in range(2)]

        slot_in = [sb(f"slot_in{i}", [P, ST, ROW]) for i in range(2)]
        x_split = [sb(f"x_split{i}", [P, ST, 3, C], bf16) for i in range(2)]
        x_rest = sb("x_rest", [P, ST, C])
        meta = [sb(f"meta{i}", [P, ST, 2]) for i in range(2)]
        xT = [sb(f"xT{i}", [P, 2, 4 * P], bf16) for i in range(2)]
        hid = [[sb(f"hid{p}_{i}", [P, 2, 4 * P], bf16) for i in range(2)] for p in range(3)]
        hid_rest = [sb(f"hid_rest{i}", [P, 2, 4 * P]) for i in range(2)]
        bad = sb("bad", [P, UT, C])
        neg = sb("neg", [P, UT, C])
        pos = sb("pos", [P, UT, C])
        edge = sb("edge", [P, UT, C])
        edge_free = sb("edge_free", [P, 1])
        pool_zero = sb("pool_zero", [P, 1])
        pool_tick = sb("pool_tick", [P, 1])
        ys = [sb(f"ys{i}", [P, UT, C]) for i in range(YB)]

        y_in = [x_in[i][:].rearrange("p (h t c) -> p h t c", h=2, t=TT) for i in range(2)]
        total = [sq1, xn]
        o_sb = [tile[:].rearrange("p s c -> p (s c)") for tile in (mix, sq2)]

        psX = ps("psX", [P, HW])
        psC = ps("psC", [P, HW])
        psD = ps("psD", [P, HW])
        psT = ps("psT", [P, 512])
        psM = ps("psM", [P, 512])
        psTb = psT[:].bitcast(bf16)
        p_freq = psT[0:S, 0:2 * P]
        p_col = psT[0:C, 256:258]
        p_z = psT[0:C, 258:260]
        p_cf = psM[:, 0:P]
        p_sf = psM[:, 258:258 + C]
        p_base = psM[:, 322:322 + 2 * E]
        p_sum = psM[:, 338:338 + E]
        p_log = psM[:, 384:384 + P]

        const_in = sem("const_in")
        gw_zero = sem("gw_zero")
        zero_set = sem("zero_set")
        ones_set = sem("ones_set")
        pool_ticked = sem("pool_ticked")
        weights_in = sem("weights_in")
        big_in = sem("big_in")
        setup_mm = sem("setup_mm")
        setup_done = sem("setup_done")
        empty_set = sem("empty_set")
        slot_init = sem("slot_init")
        token_init = sem("token_init")
        x_loaded = [sem(f"x_loaded{i}") for i in range(2)]
        x_centred = sem("x_centred")
        x_turned = sem("x_turned")
        squared1 = sem("squared1")
        squared2 = sem("squared2")
        xn_done = sem("xn_done")
        mean_done = sem("mean_done")
        col_mm = sem("col_mm")
        col_done = sem("col_done")
        freq_mm = sem("freq_mm")
        freq_done = sem("freq_done")
        cf_mm = sem("cf_mm")
        cf_exp_done = sem("cf_exp_done")
        sf_mm = sem("sf_mm")
        sf_read = sem("sf_read")
        cf_col_done = sem("cf_col_done")
        colb_done = sem("colb_done")
        cf_read = sem("cf_read")
        var1_done = sem("var1_done")
        var2_done = sem("var2_done")
        x1_done = sem("x1_done")
        x1_kept = sem("x1_kept")
        x1_turned = sem("x1_turned")
        x1T_done = sem("x1T_done")
        x1_centred = sem("x1_centred")
        logits_mm = sem("logits_mm")
        logits_read = sem("logits_read")
        below_done = sem("below_done")
        exp_done = sem("exp_done")
        numbered = sem("numbered")
        run_done = sem("run_done")
        base_mm = sem("base_mm")
        base_read = sem("base_read")
        rows_done = sem("rows_done")
        slots_done = sem("slots_done")
        rows_out = [sem(f"rows_out{i}") for i in range(2)]
        dve_step = sem("dve_step")
        slot_loaded = [sem(f"slot_loaded{i}") for i in range(2)]
        w_loaded = [sem(f"w_loaded{i}") for i in range(2)]
        parts_done = sem("parts_done")
        parts_left = sem("parts_left")
        parts_kept = sem("parts_kept")
        x_part1 = sem("x_part1")
        x_left = sem("x_left")
        x_part2 = sem("x_part2")
        x_part3 = sem("x_part3")
        meta_done = sem("meta_done")
        slots_turned = sem("slots_turned")
        xT_done = sem("xT_done")
        hid_mm = sem("hid_mm")
        hid_part1 = sem("hid_part1")
        hid_left = sem("hid_left")
        hid_part2 = sem("hid_part2")
        hid_part3 = sem("hid_part3")
        y_mm = sem("y_mm")
        y_read = sem("y_read")
        y_done = sem("y_done")
        y_out = [sem(f"y_out{i}") for i in range(YB)]
        y_loaded = [sem(f"y_loaded{i}") for i in range(2)]
        total_done = sem("total_done")
        out_turned = sem("out_turned")
        out_copied = sem("out_copied")
        stored = [sem(f"stored{i}") for i in range(2)]

        N_CONST = 2 * 16
        N_WEIGHTS = 5 * 16
        N_BIG = 5 * 16
        N_SETUP = 3
        FIRST_STEPS = 14
        TURN_STEPS = 29
        LAST_STEPS = 25
        SET_STEPS = 3
        A_STEPS = SET_STEPS + FIRST_STEPS + (NG - 1) * TURN_STEPS + LAST_STEPS

        def wait_past(engine, semaphore, value):
            if not isinstance(value, int) or value > 0:
                engine.wait_ge(semaphore, value)

        def each_turn(engine, body):
            body(Turn(0, 0, back=False))
            body(Turn(0, 1))
            body(Turn(0, 2))
            with engine.Fori(1, NG // 2 - 1) as k:
                for o in range(2):
                    body(Turn(k, 1 + o))
            body(Turn(0, NG - 1, ahead=False))
            body(Turn(0, NG, front=False, ahead=False))

        def each_pair(engine, body):
            body(0, False)
            with engine.Fori(1, E // 2 - 1) as k:
                body(k, False)
            body(E // 2 - 1, True)

        block = ctx.enter_context(nc.Block())

        @block.sync
        def _(sp):
            sp.dma_start(kc[:], const).then_inc(const_in, 16)
            sp.dma_start(dft_cols[:], dft.rearrange("k (a n) -> k a n", a=8)).then_inc(const_in, 16)
            for g in range(2):
                sp.dma_start(x_in[g][:], x_rows[g * P:(g + 1) * P, :]).then_inc(x_loaded[g], 16)
            sp.dma_start(gb8[:], gate_b.partition_broadcast(P)).then_inc(weights_in, 16)
            sp.dma_start(cw[:], conv_w).then_inc(weights_in, 16)
            sp.dma_start(cb[:], conv_b.rearrange("(a n) -> a n", a=1)).then_inc(weights_in, 16)
            sp.wait_ge(gw_zero, 1)
            for h in range(2):
                sp.dma_start(gw[h * C:(h + 1) * C, h * E:(h + 1) * E], gate_w).then_inc(weights_in, 16)
            sp.wait_ge(empty_set, 2)
            for e in range(E):
                sp.dma_start(slot_rows[e * CAP:(e + 1) * CAP, :].rearrange("(p j) c -> p j c", p=P),
                             empty_row[:]).then_inc(slot_init, 16)
            for g in range(NG):
                sp.dma_start(token_out[g * S * P:(g + 1) * S * P, :].rearrange("(p j) c -> p j c", p=P),
                             zero_row[:]).then_inc(token_init, 16)
            for h in range(2):
                sp.dma_start(w1_all[h * C:(h + 1) * C, :, :], w1.rearrange("e d f -> d e f")).then_inc(big_in, 16)
            sp.dma_start(w2_all[:].rearrange("f e h c -> f (e h) c"),
                         w2.rearrange("e (h f) c -> f (e h) c", h=2)).then_inc(big_in, 16)
            sp.dma_start(bias_all[:, 0:F], b1).then_inc(big_in, 16)
            sp.dma_start(bias_all[:, F:], b2).then_inc(big_in, 16)
            with sp.Fori(0, NG // 2 - 1) as k:
                for u in range(2):
                    sp.wait_ge(x_turned, 2 * k + u + 1)
                    sp.dma_start(x_in[u][:], x_rows[bass.ds((2 * k + u + 2) * P, P), :]).then_inc(x_loaded[u], 16)

            sp.wait_ge(parts_done, 1)
            sp.wait_ge(parts_left, 4)
            sp.dma_start(w_parts.rearrange("e p n -> p e n"), wp_all[:]).then_inc(parts_kept, 16)
            sp.dma_start(b_parts.rearrange("a e n -> e a n"), bp_all[:]).then_inc(parts_kept, 16)

            def load_slots(k, u):
                sp.dma_start(slot_in[u][:], slot_rows[bass.ds((2 * k + u) * CAP, CAP), :]
                             .rearrange("(p j) c -> p j c", p=P)).then_inc(slot_loaded[u], 16)

            def load_weights(k, u):
                e = 2 * k + u
                sp.dma_start(wp[u][:], w_parts[bass.ds(e, 1), :, :].rearrange("a p n -> (a p) n")).then_inc(w_loaded[u], 16)
                sp.dma_start(bp[u][:], b_parts[:, bass.ds(e, 1), :].rearrange("p a n -> p (a n)")).then_inc(w_loaded[u], 16)

            for u in range(2):
                sp.wait_ge(rows_out[u], NG // 2 * S * 16)
            load_slots(0, 0)
            sp.wait_ge(parts_kept, 32)
            load_weights(0, 0)
            load_slots(0, 1)
            load_weights(0, 1)
            with sp.Fori(0, E // 2 - 1) as k:
                for u in range(2):
                    sp.wait_ge(meta_done, 2 * k + u + 1)
                    load_slots(k + 1, u)
                    sp.wait_ge(y_mm, (2 * k + u + 1) * NU)
                    load_weights(k + 1, u)

            def load_y(g, u):
                sp.dma_start(y_in[u], token_out[bass.ds(g * S * P, S * P), :]
                             .rearrange("(h p t) c -> p h t c", h=2, p=P)).then_inc(y_loaded[u], 16)

            for b in range(YB):
                sp.wait_ge(y_out[b], E * UT * 16)
            for u in range(2):
                load_y(u, u)
            with sp.Fori(0, NG // 2 - 1) as k:
                for u in range(2):
                    sp.wait_ge(total_done, 2 * k + u + 1)
                    load_y(2 * k + u + 2, u)
            for u in range(2):
                sp.wait_ge(stored[u], NG // 2 * 16)

        @block.gpsimd
        def _(pool):

            pool.wait_ge(zero_set, 1)
            pool.wait_ge(slot_init, E * 16)

            def tick():
                nc.gpsimd.tensor_tensor(pool_tick[:], pool_zero[:], pool_zero[:], ALU.add).then_inc(pool_ticked, 1)

            def dispatch(T):
                G = T.back
                if G is None:
                    return
                wait_past(pool, pool_ticked, G.g)
                pool.wait_ge(slots_done, G.g + 1)
                pool.wait_ge(rows_done, G.g + 1)
                pool.wait_ge(numbered, G.g + 1)
                tick()
                for s in range(S):
                    pool.indirect_dma_start(
                        out=slot_rows, out_offset=bass.IndirectOffsetOnAxis(ap=slots[G.u][:, s:s + 1], axis=0),
                        in_=rows[G.u][:, s, :], in_offset=None,
                        bounds_check=SLOTS - 1, oob_is_err=False).then_inc(rows_out[G.u], 16)

            each_turn(pool, dispatch)
            pool.wait_ge(token_init, NG * 16)
            with pool.Fori(0, E // 2) as k:
                for local in range(2 * NU):
                    u, j = local // NU, local % NU
                    pool.wait_ge(pool_ticked, 2 * NU * k + local + NG)
                    pool.wait_ge(y_done, 2 * NU * k + local + 1)
                    tick()
                    ids = meta[u][:].bitcast(u32)
                    for i in range(UT):
                        n = UT * j + i
                        pool.indirect_dma_start(
                            out=token_out, out_offset=bass.IndirectOffsetOnAxis(ap=ids[:, n, 1:2], axis=0),
                            in_=ys[local % YB][:, i, :], in_offset=None,
                            bounds_check=NTOK - 1, oob_is_err=False).then_inc(y_out[local % YB], 16)

        @block.scalar
        def _(act):
            act.wait_ge(setup_mm, N_SETUP)
            nc.scalar.copy(cgw[:], psM[:, 0:2 * E]).then_inc(setup_done, 1)
            nc.scalar.copy(cwT[:], psM[0:C, 64:64 + C]).then_inc(setup_done, 1)
            nc.scalar.mul(ncb[:], psM[0:C, 128:129], -1.0).then_inc(setup_done, 1)

            def square_ahead(G):
                act.wait_ge(x_centred, G.g + 1)
                wait_past(act, var1_done, G.g)
                nc.scalar.activation(sq1[:].rearrange("p s c -> p (s c)"), psC[:], ACT.Square).then_inc(squared1, 1)

            def a_turn(T):
                i = T.i
                if T.front:
                    act.wait_ge(col_mm, i + 1)
                    nc.scalar.copy(col[:], p_col).then_inc(col_done, 1)
                    act.wait_ge(freq_mm, i + 1)
                    nc.scalar.copy(row_freq[:], p_freq.unsqueeze(2).to_broadcast([S, 2 * P, 4])).then_inc(freq_done, 1)
                    nc.scalar.activation(cf_exp[:], p_z, ACT.Exp, bias=ncb[:, 0:1], scale=-1.0).then_inc(cf_exp_done, 1)
                    act.wait_ge(cf_col_done, i + 1)
                    nc.scalar.copy(colb[:], cf_col[:].unsqueeze(2).to_broadcast([C, 2, P])).then_inc(colb_done, 1)
                if T.ahead:
                    square_ahead(T.ahead)
                if T.back:
                    act.wait_ge(below_done, i)
                    nc.scalar.activation(expo[:], below[:], ACT.Exp).then_inc(exp_done, 1)
                if T.front:
                    for half in range(2):
                        act.wait_ge(x1_turned, 2 * i + half + 1)
                        nc.scalar.copy(x1T[:, 512 * half:512 * (half + 1)], psT[:]).then_inc(x1T_done, 1)
                    for half in range(2):
                        act.wait_ge(x1_centred, 2 * i + half + 1)
                        wait_past(act, var2_done, i)
                        nc.scalar.activation(sq2[:, 8 * half:8 * half + 8, :].rearrange("p s c -> p (s c)"),
                                             psD[:, 512 * half:512 * (half + 1)], ACT.Square).then_inc(squared2, 1)
                    nc.scalar.copy(x1_all[:, bass.ds(i, 1), :].rearrange("p a n -> p (a n)"),
                                   x1[:].rearrange("p s c -> p (s c)")).then_inc(x1_kept, 1)

            square_ahead(Group(0, 0))
            each_turn(act, a_turn)

            act.wait_ge(big_in, N_BIG)
            w1p = wp_all[:, :, 0:W1P].rearrange("p e (a f) -> p e a f", a=3)
            w2p = wp_all[:, :, W1P:].rearrange("p e (h a c) -> p e h a c", h=2, a=3)
            w2f = w2_all[:]
            nc.scalar.copy(w1p[:, :, 0, :], w1_all[:])
            nc.scalar.copy(w1p[C:P, :, 2, :], w1_all[C:P, :, :])
            nc.scalar.copy(w2p[:, :, :, 0, :], w2f)
            nc.scalar.copy(bp_all[:, 0, :], bias_all[:]).then_inc(parts_done, 1)
            act.wait_ge(parts_left, 3)
            nc.scalar.copy(w1p[:, :, 1, :], w1_all[:])
            nc.scalar.copy(w2p[:, :, :, 1, :], w2f)
            nc.scalar.copy(bp_all[:, 1, :], bias_all[:]).then_inc(parts_done, 1)

            def split_slots(k, u, part):
                if part == 1:
                    act.wait_ge(slot_loaded[u], 16 * (k + 1))
                    wait_past(act, slots_turned, (2 * k + u - 1) * NU)
                    nc.scalar.copy(x_split[u][:, :, 1, :], slot_in[u][:, :, 0:C]).then_inc(x_part1, 1)
                else:
                    act.wait_ge(x_left, 2 * k + u + 1)
                    nc.scalar.copy(x_split[u][:, :, 0, :], x_rest[:]).then_inc(x_part2, 1)

            def take_turned(k, local):
                k, local, n, e, u, j, w = unit_at(k, local)
                act.wait_ge(slots_turned, n + 1)
                wait_past(act, hid_mm, n - 1)
                nc.scalar.copy(xT[w][:].rearrange("p a n -> p (a n)"), psTb).then_inc(xT_done, 1)

            def relu(k, local):
                k, local, n, e, u, j, w = unit_at(k, local)
                act.wait_ge(hid_mm, n + 1)
                wait_past(act, y_mm, n - 1)
                nc.scalar.activation(hid[0][w][:].rearrange("p a n -> p (a n)"), (psX, psC)[w][:],
                                     ACT.Relu).then_inc(hid_part1, 1)

            def second_part(k, local):
                k, local, n, e, u, j, w = unit_at(k, local)
                act.wait_ge(hid_left, n + 1)
                nc.scalar.copy(hid[1][w][:], hid_rest[w][:]).then_inc(hid_part2, 1)

            split_slots(0, 0, 1)
            split_slots(0, 0, 2)
            take_turned(0, 0)
            take_turned(0, 1)
            relu(0, 0)

            def pair(k, last):
                for local in range(2 * NU):
                    second_part(k, local)
                    if not last or local + 1 < 2 * NU:
                        relu(k, local + 1)
                    if not last or local + 2 < 2 * NU:
                        take_turned(k, local + 2)
                    nk, nu = (k, 1) if local < NU else (k + 1, 0)
                    if local % NU in (0, 2) and not (last and local >= NU):
                        split_slots(nk, nu, 1 + (local % NU) // 2)

            each_pair(act, pair)

            def c_group(G):
                act.wait_ge(out_turned, G.g + 1)
                nc.scalar.copy(o_sb[G.u].rearrange("q (p t) -> q t p", t=TT),
                               (psX, psC)[G.u][:].rearrange("q (t p) -> q t p", t=TT)).then_inc(out_copied, 1)
                act.wait_ge(out_copied, G.g + 1)
                act.dma_start(out_rows[bass.ds(G.g * P, P), :], o_sb[G.u]).then_inc(stored[G.u], 16)

            for g in range(2):
                c_group(Group(0, g))
            with act.Fori(1, NG // 2) as k:
                for o in range(2):
                    act.wait_ge(stored[o], k * 16)
                    c_group(Group(k, o))

        @block.vector
        def _(dve):
            nc.vector.memset(gw[:], 0.0).then_inc(gw_zero, 1)
            nc.vector.memset(zero_row[:], 0.0).then_inc(empty_set, 1)
            nc.vector.memset(empty_row[:], 1.0).then_inc(empty_set, 1)
            nc.vector.memset(pool_zero[:], 0.0).then_inc(zero_set, 1)
            nc.vector.memset(carry[:], 0.0).then_inc(dve_step, 1)
            dve.wait_ge(weights_in, N_WEIGHTS)
            nc.vector.tensor_copy(gb[:], gb8[:].unsqueeze(1).unsqueeze(3).to_broadcast([P, 2, E, TT])).then_inc(dve_step, 1)
            dve.wait_ge(const_in, N_CONST)
            nc.vector.tensor_copy(token_f[:], token_of).then_inc(dve_step, 1)
            nc.vector.memset(ones3[:], 1.0).then_inc(ones_set, 1)
            nc.vector.tensor_copy(ident_b[:], ident).then_inc(ones_set, 1)
            dve.wait_ge(dve_step, SET_STEPS)

            class Steps:

                def __init__(self, base):
                    self.base, self.n = base, 0

                def done(self, instruction):
                    instruction.then_inc(dve_step, 1)
                    self.n += 1
                    return self.n

                def wait(self, n):
                    dve.wait_ge(dve_step, self.base + n)

            def inverse_roots(st, part):
                v, y, q = vv[:, part, :], rstd[:, part, :], nq[:, part, :]
                st.wait(st.done(nc.vector.tensor_scalar(y.bitcast(i32), v.bitcast(i32), -0.5, RSQRT_SEED,
                                                        ALU.mult, ALU.add)))
                for _ in range(3):
                    st.wait(st.done(nc.vector.tensor_tensor(q, y, y, ALU.mult)))
                    st.wait(st.done(nc.vector.scalar_tensor_tensor(q, q, -0.5, v, ALU.mult, ALU.mult)))
                    st.wait(st.done(nc.vector.scalar_tensor_tensor(y, q, 1.5, y, ALU.add, ALU.mult)))

            def over_c(tile):
                return tile.unsqueeze(2).to_broadcast([P, S, C])

            def thc(tile):
                return tile.rearrange("p (t h) c -> p t h c", h=2)

            def ht_e(tile):
                return tile[:].rearrange("p h e t -> p h t e")

            def th(tile):
                return tile[:].rearrange("p (t h) -> p h t", h=2)

            def over_e(tile):
                return th(tile).unsqueeze(2).to_broadcast([P, 2, E, TT])

            def a_turn(T):
                if isinstance(T.i, int) and T.i == 0:
                    st = Steps(SET_STEPS)
                else:
                    st = Steps(SET_STEPS + FIRST_STEPS + TURN_STEPS * (T.i - 1))
                i = T.i
                if T.front:
                    dve.wait_ge(squared1, i + 1)
                    nc.vector.tensor_reduce(vv[:, 0, :], sq1[:], AX.X, ALU.add).then_inc(var1_done, 1)
                if T.back:
                    dve.wait_ge(squared2, 2 * i)
                    nc.vector.tensor_reduce(vv[:, 1, :], sq2[:], AX.X, ALU.add).then_inc(var2_done, 1)
                if T.front:
                    dve.wait_ge(var1_done, i + 1)
                    eps = st.done(nc.vector.tensor_scalar(vv[:, 0, :], vv[:, 0, :], 1.0 / C, 1e-6, ALU.mult, ALU.add))
                if T.back:
                    dve.wait_ge(var2_done, i)
                    eps = st.done(nc.vector.tensor_scalar(vv[:, 1, :], vv[:, 1, :], 1.0 / C, 1e-5, ALU.mult, ALU.add))
                st.wait(eps)
                inverse_roots(st, slice(0 if T.front else 1, 2 if T.back else 1))
                if T.front:
                    nc.vector.tensor_tensor(xn[:], psC[:].rearrange("p (s c) -> p s c", c=C), over_c(rstd[:, 0, :]),
                                            ALU.mult).then_inc(xn_done, 1)
                    dve.wait_ge(xn_done, i + 1)
                    nc.vector.tensor_reduce(mean_n[:], xn[:], AX.X, ALU.add).then_inc(mean_done, 1)
                if T.back:
                    u = T.back.u
                    wait_past(dve, rows_out[u], T.back.half * S * 16)
                    nc.vector.tensor_tensor(rows[u][:, :, 0:C], psD[:].rearrange("p (s c) -> p s c", c=C),
                                            over_c(rstd[:, 1, :]), ALU.mult).then_inc(rows_done, 1)
                    dve.wait_ge(logits_mm, i)
                    nc.vector.tensor_tensor(
                        lg[:].rearrange("p h e t -> p t h e"), p_log.rearrange("p (t h e) -> p t h e", t=TT, h=2),
                        rstd[:, 1, :].rearrange("p (t h) -> p t h", h=2).unsqueeze(3).to_broadcast([P, TT, 2, E]),
                        ALU.mult).then_inc(logits_read, 1)
                if T.front:
                    dve.wait_ge(cf_exp_done, i + 1)
                    st.wait(st.done(nc.vector.tensor_scalar(cf_den[:], cf_exp[:], 1.0, None, ALU.add)))
                    nc.vector.reciprocal(cf_col[:], cf_den[:]).then_inc(cf_col_done, 1)
                if T.back:
                    nc.vector.tensor_copy(rows[u][:].bitcast(u32)[:, :, C + 1], token_f[:]).then_inc(numbered, 1)
                    dve.wait_ge(logits_read, i)
                    st.wait(st.done(nc.vector.tensor_tensor(lgb[:], lg[:], gb[:], ALU.add)))
                    st.wait(st.done(nc.vector.tensor_reduce(th(top), ht_e(lgb), AX.X, ALU.max)))
                    nc.vector.tensor_tensor(below[:], lgb[:], over_e(top), ALU.subtract).then_inc(below_done, 1)
                    dve.wait_ge(numbered, i)
                    numbers = st.done(nc.vector.tensor_scalar(token_f[:], token_f[:], float(S * P), None, ALU.add))
                    dve.wait_ge(below_done, i)
                    st.wait(st.done(nc.vector.scalar_tensor_tensor(
                        cand[:].rearrange("p h e t -> p (h e t)"), below[:].rearrange("p h e t -> p (h e t)"), 0.0,
                        e_less_8, ALU.is_equal, ALU.mult)))
                    st.wait(st.done(nc.vector.tensor_reduce(th(pick), ht_e(cand), AX.X, ALU.min)))
                    st.wait(st.done(nc.vector.tensor_tensor(hot[:], cand[:], over_e(pick), ALU.is_equal)))
                    nc.vector.tensor_tensor_scan(run[:].rearrange("p h e t -> p (h e t)"), scan_keep,
                                                 hot[:].rearrange("p h e t -> p (h e t)"), 0.0,
                                                 ALU.mult, ALU.add).then_inc(run_done, 1)
                if T.front:
                    dve.wait_ge(sf_mm, i + 1)
                    nc.vector.tensor_tensor(
                        sf_all[:], p_sf.rearrange("p (h q t) -> p h q t", h=2, q=4),
                        own_q.unsqueeze(1).unsqueeze(3).to_broadcast([P, 2, 4, TT]), ALU.mult).then_inc(sf_read, 1)
                    dve.wait_ge(sf_read, i + 1)
                    st.wait(st.done(nc.vector.tensor_reduce(th(sf), sf_all[:].rearrange("p h q t -> p h t q"),
                                                            AX.X, ALU.add)))
                    dve.wait_ge(cf_mm, i + 1)
                    nc.vector.tensor_tensor(
                        thc(mix[:]), p_cf.rearrange("p (h c) -> p h c", h=2).unsqueeze(1).to_broadcast([P, TT, 2, C]),
                        thc(over_c(sf[:])), ALU.add).then_inc(cf_read, 1)
                    dve.wait_ge(cf_read, i + 1)
                    mixed = st.done(nc.vector.tensor_tensor(mix[:], mix[:], xn[:], ALU.mult))
                if T.back:
                    dve.wait_ge(exp_done, i)
                    st.wait(st.done(nc.vector.tensor_reduce(th(den), ht_e(expo), AX.X, ALU.add)))
                    prob = st.done(nc.vector.reciprocal(rows[u][:, :, C], den[:]))
                if T.front:
                    st.wait(mixed)
                    dve.wait_ge(x_turned, i + 1)
                    wait_past(dve, x1_kept, i)
                    nc.vector.tensor_tensor(x1[:], mix[:], psX[:].rearrange("p (s c) -> p s c", c=C),
                                            ALU.add).then_inc(x1_done, 1)
                if T.back:
                    dve.wait_ge(base_mm, i)
                    st.wait(st.done(nc.vector.tensor_tensor(
                        start[:], p_base.rearrange("p (h e) -> p h e", h=2),
                        carry[:].unsqueeze(1).to_broadcast([P, 2, E]), ALU.add)))
                    nc.vector.tensor_tensor(carry[:], carry[:], p_sum, ALU.add).then_inc(base_read, 1)
                    st.wait(st.done(nc.vector.tensor_tensor(
                        place[:], run[:], start[:].unsqueeze(3).to_broadcast([P, 2, E, TT]), ALU.add)))
                    st.wait(st.done(nc.vector.tensor_tensor(own[:], place[:], hot[:], ALU.mult)))
                    st.wait(st.done(nc.vector.tensor_reduce(th(rank), ht_e(own), AX.X, ALU.add)))
                    st.done(nc.vector.scalar_tensor_tensor(slot_f[:], pick[:], float(CAP), rank[:], ALU.mult, ALU.add))
                    st.wait(st.done(nc.vector.tensor_scalar(over[:], rank[:], float(CAP), float(1 << 20),
                                                            ALU.is_gt, ALU.mult)))
                    st.wait(prob)
                    st.wait(numbers)
                    nc.vector.scalar_tensor_tensor(slots[u][:], slot_f[:], float(E * CAP - 1), over[:], ALU.add,
                                                   ALU.add).then_inc(slots_done, 1)
                    dve.wait_ge(slots_done, i)
                    dve.wait_ge(base_read, i)
                assert st.n == (FIRST_STEPS if not T.back else LAST_STEPS if not T.front else TURN_STEPS), st.n

            each_turn(dve, a_turn)

            w1p = wp_all[:, :, 0:W1P].rearrange("p e (a f) -> p e a f", a=3)
            w2p = wp_all[:, :, W1P:].rearrange("p e (h a c) -> p e h a c", h=2, a=3)
            w2f = w2_all[:]
            dve.wait_ge(parts_done, 1)
            nc.vector.tensor_tensor(w1_all[:], w1_all[:], w1p[:, :, 0, :], ALU.subtract).then_inc(parts_left, 1)
            nc.vector.tensor_tensor(w2f, w2f, w2p[:, :, :, 0, :], ALU.subtract).then_inc(parts_left, 1)
            nc.vector.tensor_tensor(bias_all[:], bias_all[:], bp_all[:, 0, :], ALU.subtract).then_inc(parts_left, 1)
            dve.wait_ge(parts_left, 3)
            dve.wait_ge(parts_done, 2)
            nc.vector.tensor_tensor(w1p[0:C, :, 2, :], w1_all[0:C, :, :], w1p[0:C, :, 1, :], ALU.subtract)
            nc.vector.tensor_tensor(w2p[:, :, :, 2, :], w2f, w2p[:, :, :, 1, :], ALU.subtract)
            nc.vector.tensor_tensor(bp_all[:, 2, :], bias_all[:], bp_all[:, 1, :], ALU.subtract).then_inc(parts_left, 1)

            def split_slots(k, u, part):
                if part == 1:
                    dve.wait_ge(x_part1, 2 * k + u + 1)
                    wait_past(dve, x_part3, 2 * k + u)
                    nc.vector.tensor_tensor(x_rest[:], slot_in[u][:, :, 0:C], x_split[u][:, :, 1, :],
                                            ALU.subtract).then_inc(x_left, 1)
                else:
                    dve.wait_ge(x_part2, 2 * k + u + 1)
                    nc.vector.tensor_tensor(x_split[u][:, :, 2, :], x_rest[:], x_split[u][:, :, 0, :],
                                            ALU.subtract).then_inc(x_part3, 1)

            def note(k, u):
                e = 2 * k + u
                dve.wait_ge(slot_loaded[u], 16 * (k + 1))
                for b in range(YB):
                    wait_past(dve, y_out[b], (e - 1) * UT * 16)
                nc.vector.tensor_copy(meta[u][:], slot_in[u][:, :, C:C + 2]).then_inc(meta_done, 1)

            def rest(k, local):
                k, local, n, e, u, j, w = unit_at(k, local)
                dve.wait_ge(hid_part1, n + 1)
                nc.vector.scalar_tensor_tensor(hid_rest[w][:].rearrange("p a n -> p (a n)"), (psX, psC)[w][:], 0.0,
                                               hid[0][w][:].rearrange("p a n -> p (a n)"), ALU.max,
                                               ALU.subtract).then_inc(hid_left, 1)

            def third_part(k, local):
                k, local, n, e, u, j, w = unit_at(k, local)
                dve.wait_ge(hid_part2, n + 1)
                nc.vector.tensor_tensor(hid[2][w][:], hid_rest[w][:], hid[1][w][:], ALU.subtract).then_inc(hid_part3, 1)

            def scaled(k, local, st):
                k, local, n, e, u, j, w = unit_at(k, local)
                b = local % YB
                y = ys[b]
                dve.wait_ge(y_mm, n + 1)
                dve.wait_ge(meta_done, e + 1)
                wait_past(dve, y_out[b], e * UT * 16)
                nc.vector.tensor_tensor(
                    y[:], psD[:, 512 * w:512 * w + UT * C].rearrange("p (i c) -> p i c", c=C),
                    meta[u][:, UT * j:UT * (j + 1), 0:1].to_broadcast([P, UT, C]), ALU.mult).then_inc(y_read, 1)

            def guard(k, local, st):
                k, local, n, e, u, j, w = unit_at(k, local)
                y = ys[local % YB]
                dve.wait_ge(y_read, n + 1)
                nc.vector.tensor_scalar(bad[:], y[:], 0.0, 0.0, ALU.mult, ALU.not_equal)
                nc.vector.tensor_scalar(neg[:], y[:], 0.0, -1e4, ALU.is_lt, ALU.mult)
                st.wait(st.done(nc.vector.tensor_scalar(pos[:], y[:], 0.0, 1e4, ALU.is_gt, ALU.mult)))
                st.wait(st.done(nc.vector.tensor_tensor(edge[:], neg[:], pos[:], ALU.add)))

            def replace(k, local):
                k, local, n, e, u, j, w = unit_at(k, local)
                flat = "p i c -> p (i c)"
                nc.vector.copy_predicated(ys[local % YB][:].rearrange(flat), bad[:].bitcast(u32).rearrange(flat),
                                          edge[:].rearrange(flat)).then_inc(y_done, 1)

            split_slots(0, 0, 1)
            split_slots(0, 0, 2)
            note(0, 0)
            rest(0, 0)

            def pair(k, last):
                for local in range(2 * NU):
                    n = 2 * NU * k + local
                    st = Steps(A_STEPS + 2 * (n - 1))
                    before_first = isinstance(k, int) and k == 0 and local == 0
                    back_k, back = (k, local - 1) if local else (k - 1, 2 * NU - 1)
                    if not before_first:
                        scaled(back_k, back, st)
                    third_part(k, local)
                    if not before_first:
                        guard(back_k, back, st)
                    if not last or local + 1 < 2 * NU:
                        rest(k, local + 1)
                    else:
                        nc.vector.memset(edge_free[:], 0.0)
                    if not before_first:
                        replace(back_k, back)
                    nk, nu = (k, 1) if local < NU else (k + 1, 0)
                    if not (last and local >= NU):
                        if local % NU == 1:
                            split_slots(nk, nu, 1)
                        if local % NU == 2:
                            split_slots(nk, nu, 2)
                        if local % NU == 4:
                            note(nk, nu)

            each_pair(dve, pair)
            k, local = E // 2 - 1, 2 * NU - 1
            st = Steps(A_STEPS + 2 * (E * NU - 1))
            scaled(k, local, st)
            guard(k, local, st)
            nc.vector.memset(edge_free[:], 0.0)
            replace(k, local)

            def c_group(G):
                dve.wait_ge(y_loaded[G.u], 16 * (G.half + 1))
                wait_past(dve, out_turned, G.g - 1)
                nc.vector.tensor_tensor(
                    total[G.u][:].rearrange("p (t h) c -> p h t c", h=2),
                    x1_all[:, bass.ds(G.g, 1), :].rearrange("p a (t h c) -> p (a h) t c", t=TT, h=2),
                    y_in[G.u], ALU.add).then_inc(total_done, 1)

            for g in range(2):
                dve.wait_ge(y_loaded[g], 16)
                nc.vector.tensor_tensor(
                    total[g][:].rearrange("p (t h) c -> p h t c", h=2),
                    x1_all[:, g, :].rearrange("p (t h c) -> p h t c", t=TT, h=2),
                    y_in[g], ALU.add).then_inc(total_done, 1)
            with dve.Fori(1, NG // 2) as k:
                for o in range(2):
                    c_group(Group(k, o))

        @block.tensor
        def _(pe):
            pe.wait_ge(const_in, N_CONST)
            pe.wait_ge(weights_in, N_WEIGHTS)
            nc.tensor.matmul(psM[:, 0:2 * E], centre, gw[:], start=True, stop=True).then_inc(setup_mm, 1)
            nc.tensor.transpose(psM[0:C, 64:64 + C], cw[:], ident[0:C, 0:C]).then_inc(setup_mm, 1)
            nc.tensor.matmul(psM[0:C, 128:129], cb[:], ones[0:1, 0:1], start=True, stop=True).then_inc(setup_mm, 1)
            pe.wait_ge(setup_done, N_SETUP)

            def pixels(G):
                return x_in[G.u][:].rearrange("q (p t) -> q t p", t=TT)

            def centre_ahead(G):
                pe.wait_ge(x_loaded[G.u], 16 * (G.half + 1))
                wait_past(pe, xn_done, G.g)
                for t in range(TT):
                    last = nc.tensor.matmul(psC[:, t * P:(t + 1) * P], pixels(G)[:, t, :], centre, start=True, stop=True)
                last.then_inc(x_centred, 1)

            def turn_ahead(G):
                wait_past(pe, x1_done, G.g)
                for t in range(TT):
                    last = nc.tensor.transpose(psX[:, t * P:(t + 1) * P], pixels(G)[:, t, :], ident)
                last.then_inc(x_turned, 1)

            def a_turn(T):
                i = T.i
                if T.front:
                    pe.wait_ge(xn_done, i + 1)
                    wait_past(pe, x1T_done, 2 * i)
                    for h in range(2):
                        last = nc.tensor.matmul(p_col[:, h:h + 1], xn[0:1, h, :], ones[0:1, 0:1], start=True, stop=True)
                    last.then_inc(col_mm, 1)
                    pe.wait_ge(mean_done, i + 1)
                    pe.wait_ge(col_done, i + 1)
                    nc.tensor.matmul(p_freq, mean_n[:], dft_rows, start=True, stop=True)
                    nc.tensor.matmul(p_z, cwT[:], col[:], start=True, stop=True).then_inc(freq_mm, 1)
                    pe.wait_ge(freq_done, i + 1)
                    wait_past(pe, logits_read, i)
                    for a in range(8):
                        last = nc.tensor.matmul(p_sf, row_freq[:, a * 32:(a + 1) * 32, :].rearrange("k r q -> k (r q)"),
                                                dft_cols[:, a, :], start=(a == 0), stop=(a == 7))
                    last.then_inc(sf_mm, 1)
                if T.ahead:
                    centre_ahead(T.ahead)
                if T.front:
                    pe.wait_ge(colb_done, i + 1)
                    pe.wait_ge(sf_read, i + 1)
                    for h in range(2):
                        last = nc.tensor.matmul(p_cf[:, h * C:(h + 1) * C], colb[:, h, :], ident[0:C, 0:C],
                                                start=True, stop=True)
                    last.then_inc(cf_mm, 1)
                if T.back:
                    pe.wait_ge(run_done, i)
                    if T.front:
                        pe.wait_ge(cf_read, i + 1)
                    else:
                        pe.wait_ge(logits_read, i)
                    counts = run[:].rearrange("p h e t -> p (h e) t")[:, :, TT - 1]
                    nc.tensor.matmul(p_base[:, 0:E], before, counts[:, 0:E], start=True, stop=True)
                    nc.tensor.matmul(p_base[:, E:], before, counts[:, E:], start=True, stop=False)
                    nc.tensor.matmul(p_base[:, E:], ones, counts[:, 0:E], start=False, stop=True)
                    nc.tensor.matmul(p_sum, ones, counts[:, 0:E], start=True, stop=False)
                    nc.tensor.matmul(p_sum, ones, counts[:, E:], start=False, stop=True).then_inc(base_mm, 1)
                if T.front:
                    pe.wait_ge(x1_done, i + 1)
                    pe.wait_ge(cf_exp_done, i + 1)

                    def turn_half(half):
                        for a in range(TT // 2):
                            t = half * TT // 2 + a
                            last = nc.tensor.transpose(psT[:, a * P:(a + 1) * P],
                                                       x1[:, 2 * t:2 * t + 2, :].rearrange("p s c -> p (s c)"), ident)
                        last.then_inc(x1_turned, 1)

                    def centre_half(half):
                        for t in range(half * TT // 2, (half + 1) * TT // 2):
                            last = nc.tensor.matmul(psD[:, t * P:(t + 1) * P], x1T[:, t * P:(t + 1) * P], centre,
                                                    start=True, stop=True)
                        last.then_inc(x1_centred, 1)

                    turn_half(0)
                    pe.wait_ge(x1T_done, 2 * i + 1)
                    turn_half(1)
                    wait_past(pe, rows_done, i)
                    centre_half(0)
                    pe.wait_ge(x1T_done, 2 * i + 2)
                    centre_half(1)
                    wait_past(pe, base_read, i)
                    pe.wait_ge(cf_read, i + 1)
                    for t in range(TT):
                        last = nc.tensor.matmul(p_log[:, t * 2 * E:(t + 1) * 2 * E], x1T[:, t * P:(t + 1) * P], cgw[:],
                                                start=True, stop=True)
                    last.then_inc(logits_mm, 1)
                if T.ahead:
                    turn_ahead(T.ahead)

            centre_ahead(Group(0, 0))
            turn_ahead(Group(0, 0))
            each_turn(pe, a_turn)

            def turn(k, local):
                k, local, n, e, u, j, w = unit_at(k, local)
                if j == 0:
                    pe.wait_ge(x_part3, e + 1)
                wait_past(pe, xT_done, n)
                for kind in range(2):
                    for i in range(UT):
                        at = 512 * kind + P * i
                        last = nc.tensor.transpose(psTb[:, at:at + P],
                                                   x_split[u][:, UT * j + i, kind:kind + 2, :]
                                                   .rearrange("p a c -> p (a c)"), ident_b[:])
                last.then_inc(slots_turned, 1)

            def up(k, local):
                k, local, n, e, u, j, w = unit_at(k, local)
                if j == 0:
                    pe.wait_ge(w_loaded[u], 32 * (k + 1))
                pe.wait_ge(xT_done, n + 1)
                wait_past(pe, hid_left, n - 1)
                for half in range(2):
                    o = (psX, psC)[w][:, 512 * half:512 * (half + 1)]
                    nc.tensor.matmul(o, bp[u][:, P * half:P * (half + 1)], ones3[:], start=True, stop=False)
                    for part in range(3):
                        at = F * part + P * half
                        last = nc.tensor.matmul(o, wp[u][:, at:at + P], xT[w][:, part // 2, :],
                                                start=False, stop=(part == 2))
                last.then_inc(hid_mm, 1)

            def down(k, local):
                k, local, n, e, u, j, w = unit_at(k, local)
                pe.wait_ge(hid_part3, n + 1)
                wait_past(pe, y_read, n - 1)
                for i in range(UT):
                    o = psD[:, 512 * w + C * i:512 * w + C * (i + 1)]
                    nc.tensor.matmul(o, ones3[:, 0:P], bp[u][:, F:], start=True, stop=False)
                    for half in range(2):
                        for hp in range(3):
                            for p in range(3 - hp):
                                at = W1P + C * (3 * half + p)
                                last = nc.tensor.matmul(o, hid[hp][w][:, half, P * i:P * (i + 1)], wp[u][:, at:at + C],
                                                        start=False, stop=(half == 1 and hp == 2))
                last.then_inc(y_mm, 1)

            pe.wait_ge(ones_set, 2)
            turn(0, 0)
            turn(0, 1)
            up(0, 0)

            def pair(k, last):
                for local in range(2 * NU):
                    if not last or local + 1 < 2 * NU:
                        up(k, local + 1)
                    if not last or local + 2 < 2 * NU:
                        turn(k, local + 2)
                    down(k, local)

            each_pair(pe, pair)

            def c_group(G):
                pe.wait_ge(total_done, G.g + 1)
                for t in range(TT):
                    last = nc.tensor.transpose((psX, psC)[G.u][:, t * P:(t + 1) * P],
                                               total[G.u][:, 2 * t:2 * t + 2, :].rearrange("p s c -> p (s c)"), ident)
                last.then_inc(out_turned, 1)

            for g in range(2):
                c_group(Group(0, g))
            with pe.Fori(1, NG // 2) as k:
                for o in range(2):
                    pe.wait_ge(out_copied, 2 * k + o - 1)
                    c_group(Group(k, o))


_INS = ["x", "L0_conv_W", "L0_conv_b", "L0_ffn_gate_w", "L0_ffn_gate_b", "L0_ffn_w1", "L0_ffn_b1", "L0_ffn_w2",
        "L0_ffn_b2"]


def constants():
    import numpy as np

    p = np.arange(P)
    ident = np.eye(P)
    same_half = (p[:, None] // C == p[None, :] // C)
    centre = ident - same_half / C
    before = (p[:, None] < p[None, :]).astype(float)
    ones = np.ones((P, P))
    i, q = p // 4, p % 4
    turns = 2 * np.pi / SIDE
    u = np.arange(SIDE)
    rows = np.zeros((P, 2, 4, SIDE))
    for r in range(4):
        angle = turns * np.outer(i, u)
        rows[:, 0, r, :] = np.where(q[:, None] == r, np.cos(angle), 0) / C
        rows[:, 1, r, :] = np.where(q[:, None] == r, np.sin(angle), 0) / C
    own_q = (q[:, None] == np.arange(4)[None, :]).astype(float)
    keep = np.broadcast_to(np.arange(TT) != 0, (2 * E, TT)).reshape(1, -1).repeat(P, 0).astype(float)
    e_less_8 = np.broadcast_to((np.arange(E) - E)[None, :, None], (2, E, TT)).reshape(1, -1).repeat(P, 0)
    t, h = np.arange(S) // 2, np.arange(S) % 2
    token = TT * p[:, None] + t[None, :] + HW * h[None, :]
    const = np.concatenate([ident, centre, before, ones, rows.reshape(P, -1), own_q, keep, e_less_8, token], 1)
    cols = np.zeros((S, 2, 4, 2, SIDE))
    for s in range(S):
        for r in range(4):
            angle = turns * (8 * r + t[s]) * u
            cols[s, 0, r, h[s], :] = np.cos(angle)
            cols[s, 1, r, h[s], :] = -np.sin(angle)
    return const.astype(np.float32), cols.reshape(S, -1).astype(np.float32)


def kernel(**inputs):
    import numpy as _np
    import concourse.bacc as _bacc
    from concourse import mybir as _mybir
    from concourse.bass_utils import run_bass_kernel_spmd as _run

    nc = _bacc.Bacc("TRN2", target_bir_lowering=False, num_devices=1)
    arrays, args = {}, []
    const, dft = constants()
    for name, a in [(n, inputs[n]) for n in _INS] + [("const", const), ("dft", dft)]:
        a = _np.ascontiguousarray(a)
        arrays[f"in_{name}_dram"] = a
        args.append(nc.dram_tensor(f"in_{name}_dram", a.shape, _mybir.dt.from_np(a.dtype), kind="ExternalInput").ap())
    args.append(nc.dram_tensor("out_dram", (NB, C, 32, 32), _mybir.dt.float32, kind="ExternalOutput").ap())
    build(nc, *args)
    r = _run(nc, [arrays], core_ids=[0])
    return r.results[0]["out_dram"]
```

```python
import concourse.bass as bass
from concourse import mybir
from contextlib import ExitStack

NB, C, HW = 16, 64, 1024
P = 128
NG = NB // 2
TT = HW // P
S = 2 * TT
E, F = 8, 256
NTOK = NB * HW
CAP = -(-NTOK * 5 // (4 * E))
SLOTS = E * CAP
ROW = C + 2
ST = CAP // P
UT = 4
NU = ST // UT
YG = 4
WP = 3 * F
SIDE = 32
SURE = 1


class Group:

    def __init__(self, loop, offset):
        self.g = 2 * loop + offset
        self.u = offset % 2
        self.half = loop + offset // 2


class Turn:

    def __init__(self, loop, offset, front=True, back=True, ahead=True):
        self.i = 2 * loop + offset
        self.front = Group(loop, offset) if front else None
        self.back = Group(loop, offset - 1) if back else None
        self.ahead = Group(loop, offset + 1) if ahead else None


def unit_at(k, local):
    k, local = k + local // (2 * NU), local % (2 * NU)
    return k, local, 2 * NU * k + local, 2 * k + local // NU, local // NU, local % NU, local % 2


def build(nc, x, conv_w, conv_b, gate_w, gate_b, w1, b1, w2, b2, const, dft, out):
    fp32, bf16, u32, i32 = mybir.dt.float32, mybir.dt.bfloat16, mybir.dt.uint32, mybir.dt.int32
    ALU, ACT, AX = mybir.AluOpType, mybir.ActivationFunctionType, mybir.AxisListType

    slot_rows = nc.dram_tensor("slot_rows", (SLOTS, ROW), fp32, kind="Internal").ap()
    token_out = nc.dram_tensor("token_out", (NTOK, C), fp32, kind="Internal").ap()
    w_parts = nc.dram_tensor("w_parts", (E, P, WP), bf16, kind="Internal").ap()
    x_rows = x.rearrange("b c h w -> (b c) (h w)")
    out_rows = out.rearrange("b c h w -> (b c) (h w)")

    with ExitStack() as ctx:
        def sb(name, shape, dt=fp32):
            return ctx.enter_context(nc.sbuf_tensor(name, shape, dt))

        def ps(name, shape):
            return ctx.enter_context(nc.psum_tensor(name, shape, fp32))

        def sem(name):
            return ctx.enter_context(nc.semaphore(name))

        kc = sb("kc", [P, const.shape[1]])
        at = 0
        views = []
        for width in (P, P, P, P, 2 * P, 4, P, P, S):
            views.append(kc[:, at:at + width])
            at += width
        ident, centre, before, ones, dft_rows, own_q, scan_keep, e_less_8, token_of = views
        dft_cols = sb("dft_cols", [4 * S, 2, C])
        gw = sb("gw", [P, 2 * E])
        cgw = sb("cgw", [P, 2 * E])
        gb8 = sb("gb8", [P, E])
        gb = sb("gb", [P, 2, E, TT])
        cw = sb("cw", [C, C])
        cwT = sb("cwT", [C, C])
        cb = sb("cb", [1, C])
        ncb = sb("ncb", [C, 1])
        w1_all = sb("w1_all", [P, E, F])
        b2_all = sb("b2_all", [P, E, C])
        wp_all = sb("wp_all", [P, E, WP], bf16)
        wp = [sb(f"wp{i}", [P, WP], bf16) for i in range(2)]
        w2_in = [sb(f"w2_in{i}", [P, 2, C]) for i in range(2)]
        b1_rows = sb("b1_rows", [2 * E, P])
        b1_cols = sb("b1_cols", [P, 2 * E])
        b1_in = [sb(f"b1_in{i}", [P, 2]) for i in range(2)]
        ident_b = sb("ident_b", [P, P], bf16)
        empty_row = sb("empty_row", [P, ST, ROW])
        zero_row = sb("zero_row", [P, S, C])

        x_in = [sb(f"x_in{i}", [P, HW]) for i in range(2)]
        sq1 = sb("sq1", [P, S, C])
        xn = sb("xn", [P, S, C])
        mix = sb("mix", [P, S, C])
        x1 = sb("x1", [P, S, C])
        x1_all = sb("x1_all", [P, NG, HW])
        x1T = sb("x1T", [P, HW])
        sq2 = sb("sq2", [P, S, C])
        eps = [sb(f"eps{i}", [P, 1]) for i in range(2)]
        squares = [sb(f"squares{i}", [P, S]) for i in range(2)]
        variance = [sb(f"variance{i}", [P, S]) for i in range(2)]
        logvar = [sb(f"logvar{i}", [P, S]) for i in range(2)]
        root = [sb(f"root{i}", [P, S]) for i in range(2)]
        newton = [sb(f"newton{i}", [P, S]) for i in range(2)]
        rstd = [sb(f"rstd{i}", [P, S]) for i in range(2)]
        mean_n = sb("mean_n", [P, S])
        col = sb("col", [C, 2])
        colb = sb("colb", [C, 2, P])
        mean_q = sb("mean_q", [P, 4, S])
        row_freq = sb("row_freq", [4 * S, 2 * P])
        cf_exp = sb("cf_exp", [C, 2])
        cf_den = sb("cf_den", [C, 2])
        cf_col = sb("cf_col", [C, 2])
        sf_all = sb("sf_all", [P, 2, 4, TT])
        sf = sb("sf", [P, S])
        lg = sb("lg", [P, 2, E, TT])
        lgb = sb("lgb", [P, 2, E, TT])
        top = sb("top", [P, S])
        below = sb("below", [P, 2, E, TT])
        cand = sb("cand", [P, 2, E, TT])
        expo = sb("expo", [P, 2, E, TT])
        den = sb("den", [P, S])
        pick = sb("pick", [P, S])
        hot = sb("hot", [P, 2, E, TT])
        run = sb("run", [P, 2, E, TT])
        counts_held = sb("counts_held", [P, E], i32)
        carry = sb("carry", [P, E])
        start = sb("start", [P, 2, E])
        place = sb("place", [P, 2, E, TT])
        own = sb("own", [P, 2, E, TT])
        rank = sb("rank", [P, S])
        slot_f = sb("slot_f", [P, S])
        over = sb("over", [P, S])
        token_f = sb("token_f", [P, S])
        rows = [sb(f"rows{i}", [P, S, ROW]) for i in range(2)]
        slots = [sb(f"slots{i}", [P, S], u32) for i in range(2)]

        slot_in = [sb(f"slot_in{i}", [P, ST, ROW]) for i in range(2)]
        x_split = [sb(f"x_split{i}", [P, ST, 3, C], bf16) for i in range(2)]
        x_rest = sb("x_rest", [P, ST, C])
        meta = [sb(f"meta{i}", [P, ST, 2]) for i in range(2)]
        xT = [sb(f"xT{i}", [P, 2, 4 * P], bf16) for i in range(2)]
        hid = [sb(f"hid{i}", [P, 2, 4 * P]) for i in range(2)]
        with_b2 = sb("with_b2", [P, UT, C])
        bad = sb("bad", [P, UT, C])
        neg = sb("neg", [P, UT, C])
        pos = sb("pos", [P, UT, C])
        edge = sb("edge", [P, UT, C])
        edge_free = sb("edge_free", [P, 1])
        pool_mark = sb("pool_mark", [P, 1])
        ys = [sb(f"ys{i}", [P, UT, C]) for i in range(NU)]

        def flat(tile):
            return tile[:].rearrange("p s c -> p (s c)")[:, 0:HW]

        y_in = [tile.rearrange("p (h t c) -> p h t c", h=2, t=TT)
                for tile in (x_in[0][:], x_in[1][:], flat(rows[0]), flat(rows[1]))]
        total = [sq1, xn]
        o_sb = [flat(mix), flat(sq2), flat(x1), x1T[:]]

        psX = ps("psX", [P, HW])
        psC = ps("psC", [P, HW])
        psD = ps("psD", [P, HW])
        psT = ps("psT", [P, 512])
        psM = ps("psM", [P, 512])
        psTb = psT[:].bitcast(bf16)
        p_freq = psT[0:4 * S, 0:2 * P]
        p_col = psT[0:C, 256:258]
        p_z = psT[0:C, 258:260]
        p_cf = psT[:, 0:P]
        p_sf = psM[:, 0:C]
        p_log = psM[:, P:2 * P]
        p_base = psD[:, 512:512 + 2 * E]
        p_sum = psD[:, 512 + 2 * E:512 + 3 * E]

        centre_in = sem("centre_in")
        const_in = sem("const_in")
        gw_zero = sem("gw_zero")
        eps_set = sem("eps_set")
        ident_ready = sem("ident_ready")
        all_sent = sem("all_sent")
        dispatching = sem("dispatching")
        scattering = sem("scattering")
        weights_in = sem("weights_in")
        big_in = sem("big_in")
        b2_in = sem("b2_in")
        setup_mm = sem("setup_mm")
        setup_done = sem("setup_done")
        empty_set = sem("empty_set")
        slot_init = sem("slot_init")
        token_init = sem("token_init")
        x_loaded = [sem(f"x_loaded{i}") for i in range(2)]
        x_centred = sem("x_centred")
        x_turned = sem("x_turned")
        squared1 = sem("squared1")
        squared2 = sem("squared2")
        xn_done = sem("xn_done")
        mean_done = sem("mean_done")
        col_mm = sem("col_mm")
        col_done = sem("col_done")
        freq_mm = sem("freq_mm")
        freq_done = sem("freq_done")
        cf_mm = sem("cf_mm")
        cf_exp_done = sem("cf_exp_done")
        sf_mm = sem("sf_mm")
        sf_read = sem("sf_read")
        cf_col_done = sem("cf_col_done")
        colb_done = sem("colb_done")
        cf_read = sem("cf_read")
        squares_summed = [sem(f"squares_summed{i}") for i in range(2)]
        log_done = [sem(f"log_done{i}") for i in range(2)]
        root_done = [sem(f"root_done{i}") for i in range(2)]
        mean_split = sem("mean_split")
        x1_done = sem("x1_done")
        x1_kept = sem("x1_kept")
        x1_turned = sem("x1_turned")
        x1T_done = sem("x1T_done")
        x1_centred = sem("x1_centred")
        logits_mm = sem("logits_mm")
        logits_read = sem("logits_read")
        below_done = sem("below_done")
        exp_done = sem("exp_done")
        numbered = sem("numbered")
        run_done = sem("run_done")
        base_mm = sem("base_mm")
        base_read = sem("base_read")
        rows_done = sem("rows_done")
        slots_done = sem("slots_done")
        rows_out = [sem(f"rows_out{i}") for i in range(2)]
        dve_step = sem("dve_step")
        first_slots = sem("first_slots")
        slot_loaded = [sem(f"slot_loaded{i}") for i in range(2)]
        w_loaded = [sem(f"w_loaded{i}") for i in range(2)]
        parts_done = sem("parts_done")
        parts_left = sem("parts_left")
        parts_kept = sem("parts_kept")
        x_part1 = sem("x_part1")
        x_left = sem("x_left")
        x_part2 = sem("x_part2")
        x_part3 = sem("x_part3")
        meta_done = sem("meta_done")
        b1_done = sem("b1_done")
        slots_turned = sem("slots_turned")
        xT_done = sem("xT_done")
        hid_mm = sem("hid_mm")
        hid_done = sem("hid_done")
        y_mm = sem("y_mm")
        y_read = sem("y_read")
        counts_ready = sem("counts_ready")
        y_free = sem("y_free")
        y_done = sem("y_done")
        y_out = [sem(f"y_out{i}") for i in range(NU)]
        y_loaded = [sem(f"y_loaded{i}") for i in range(YG)]
        total_done = sem("total_done")
        out_turned = sem("out_turned")
        out_copied = sem("out_copied")
        stored = [sem(f"stored{i}") for i in range(YG)]

        N_CONST = 2 * 16
        N_WEIGHTS = 6 * 16
        N_BIG = 2 * 16
        N_SETUP = 4
        FIRST_STEPS = 7
        TURN_STEPS = 25
        LAST_STEPS = 18
        SET_STEPS = 4
        A_STEPS = SET_STEPS + FIRST_STEPS + (NG - 1) * TURN_STEPS - 1 + LAST_STEPS

        def wait_past(engine, semaphore, value):
            if not isinstance(value, int) or value > 0:
                engine.wait_ge(semaphore, value)

        def each_turn(engine, body):
            body(Turn(0, 0, back=False))
            body(Turn(0, 1))
            body(Turn(0, 2))
            with engine.Fori(1, NG // 2 - 1) as k:
                for o in range(2):
                    body(Turn(k, 1 + o))
            body(Turn(0, NG - 1, ahead=False))
            body(Turn(0, NG, front=False, ahead=False))

        def each_pair(engine, body):
            body(0, False)
            with engine.Fori(1, E // 2 - 1) as k:
                body(k, False)
            body(E // 2 - 1, True)

        FIRST, OTHERS = slice(0, UT), slice(UT, ST)

        def pieces(k, u, cols):
            return 2 * k + u + (1 if cols.stop == UT else 2)

        SPLIT_AT = (0, 1)

        def each_out(engine, body):
            for b in range(YG):
                body(b, 0, b)
            with engine.Fori(1, NG // YG) as k:
                for b in range(YG):
                    body(YG * k + b, k, b)

        block = ctx.enter_context(nc.Block())

        @block.sync
        def _(sp):
            sp.dma_start(kc[:, 0:2 * P], const[:, 0:2 * P]).then_inc(centre_in, 16)
            sp.dma_start(x_in[0][:], x_rows[0:P, :]).then_inc(x_loaded[0], 16)
            sp.dma_start(kc[:, 2 * P:], const[:, 2 * P:]).then_inc(const_in, 16)
            sp.dma_start(dft_cols[:], dft.rearrange("k (a n) -> k a n", a=2)).then_inc(const_in, 16)
            sp.dma_start(gb8[:], gate_b.partition_broadcast(P)).then_inc(weights_in, 16)
            sp.dma_start(cw[:], conv_w).then_inc(weights_in, 16)
            sp.dma_start(cb[:], conv_b.rearrange("(a n) -> a n", a=1)).then_inc(weights_in, 16)
            sp.dma_start(b1_rows[:], b1.rearrange("e (h f) -> (e h) f", h=2)).then_inc(weights_in, 16)
            sp.wait_ge(gw_zero, 1)
            for h in range(2):
                sp.dma_start(gw[h * C:(h + 1) * C, h * E:(h + 1) * E], gate_w).then_inc(weights_in, 16)
            sp.dma_start(x_in[1][:], x_rows[P:2 * P, :]).then_inc(x_loaded[1], 16)
            sp.wait_ge(empty_set, 2)
            for e in range(E):
                sp.dma_start(slot_rows[e * CAP:(e + 1) * CAP, :].rearrange("(p j) c -> p j c", p=P),
                             empty_row[:]).then_inc(slot_init, 16)

            def load_x(k, u):
                sp.wait_ge(x_turned, 2 * k + u + 1)
                sp.dma_start(x_in[u][:], x_rows[bass.ds((2 * k + u + 2) * P, P), :]).then_inc(x_loaded[u], 16)

            for u in range(2):
                load_x(0, u)
            for g in range(NG):
                sp.dma_start(token_out[g * S * P:(g + 1) * S * P, :].rearrange("(p j) c -> p j c", p=P),
                             zero_row[:]).then_inc(token_init, 16)
            for h in range(2):
                sp.dma_start(w1_all[h * C:(h + 1) * C, :, :], w1.rearrange("e d f -> d e f")).then_inc(big_in, 16)
            sp.dma_start(b2_all[:].rearrange("p e c -> p (e c)"),
                         b2.rearrange("e c -> (e c)").partition_broadcast(P)).then_inc(b2_in, 16)
            with sp.Fori(1, NG // 2 - 1) as k:
                for u in range(2):
                    load_x(k, u)

            sp.wait_ge(parts_done, 2)
            sp.wait_ge(parts_left, 2)
            sp.dma_start(w_parts.rearrange("e p n -> p e n"), wp_all[:]).then_inc(parts_kept, 16)

            def load_slots(k, u):
                sp.dma_start(slot_in[u][:], slot_rows[bass.ds((2 * k + u) * CAP, CAP), :]
                             .rearrange("(j p) c -> p j c", p=P)).then_inc(slot_loaded[u], 16)

            def load_weights(k, u):
                e = 2 * k + u
                sp.dma_start(wp[u][:], w_parts[bass.ds(e, 1), :, :]
                             .rearrange("a p n -> (a p) n")).then_inc(w_loaded[u], 16)
                sp.dma_start(w2_in[u][:], w2[bass.ds(e, 1), :, :]
                             .rearrange("a (h f) c -> f (a h) c", h=2)).then_inc(w_loaded[u], 16)

            sp.wait_ge(parts_kept, 16)
            for u in range(2):
                load_weights(0, u)
            for u in range(2):
                sp.wait_ge(rows_out[u], NG // 2 * S * 16)
            first = slot_rows[0:CAP, :].rearrange("(j p) c -> p j c", p=P)
            sp.dma_start(slot_in[0][:, 0:UT, :], first[:, 0:UT, :]).then_inc(first_slots, 16)
            sp.dma_start(slot_in[0][:, UT:, :], first[:, UT:, :]).then_inc(slot_loaded[0], 16)
            load_slots(0, 1)
            with sp.Fori(0, E // 2 - 1) as k:
                for u in range(2):
                    sp.wait_ge(meta_done, 2 * k + u + 1)
                    load_slots(k + 1, u)
                    sp.wait_ge(y_mm, (2 * k + u + 1) * NU)
                    load_weights(k + 1, u)

            def load_y(g, u):
                sp.dma_start(y_in[u], token_out[bass.ds(g * S * P, S * P), :]
                             .rearrange("(h p t) c -> p h t c", h=2, p=P)).then_inc(y_loaded[u], 16)

            for b in range(SURE):
                sp.wait_ge(y_out[b], E * UT * 16)
            sp.wait_ge(y_free, (NU - SURE) * E)
            for b in range(YG):
                load_y(b, b)
            with sp.Fori(1, NG // YG) as k:
                for b in range(YG):
                    sp.wait_ge(total_done, YG * (k - 1) + b + 1)
                    load_y(YG * k + b, b)
            for b in range(YG):
                sp.wait_ge(stored[b], NG // YG * 16)

        @block.gpsimd
        def _(pool):
            pool.wait_ge(slot_init, E * 16)

            def start(work):
                pool.sem_inc(work, 1)

            def dispatch(T):
                G = T.back
                if G is None:
                    return
                pool.wait_ge(slots_done, G.g + 1)
                pool.wait_ge(rows_done, G.g + 1)
                pool.wait_ge(numbered, G.g + 1)
                start(dispatching)
                for s in range(S):
                    pool.indirect_dma_start(
                        out=slot_rows, out_offset=bass.IndirectOffsetOnAxis(ap=slots[G.u][:, s:s + 1], axis=0),
                        in_=rows[G.u][:, s, :], in_offset=None,
                        bounds_check=SLOTS - 1, oob_is_err=False).then_inc(rows_out[G.u], 16)

            each_turn(pool, dispatch)
            nc.gpsimd.memset(pool_mark[:], 0.0).then_inc(all_sent, 1)
            pool.wait_ge(token_init, NG * 16)
            pool.wait_ge(counts_ready, 1)
            sent = {b: pool.alloc_register(f"sent{b}") for b in range(SURE, NU)}
            for b in sent:
                pool.reg_mov(sent[b], 0)

            def landed(b):
                pool.wait_ge(y_out[b], sent[b])
                pool.sem_inc(y_free, 1)

            def pair(k, last):
                for local in range(2 * NU):
                    u, b = local // NU, local % NU
                    pool.wait_ge(y_done, 2 * NU * k + local + 1)
                    start(scattering)
                    ids = meta[u][:].bitcast(u32)

                    def scatter(i):
                        pool.indirect_dma_start(
                            out=token_out, out_offset=bass.IndirectOffsetOnAxis(ap=ids[:, UT * b + i, 1:2], axis=0),
                            in_=ys[b][:, i, :], in_offset=None,
                            bounds_check=NTOK - 1, oob_is_err=False).then_inc(y_out[b], 16)
                        if b >= SURE:
                            pool.reg_add(sent[b], sent[b], 16)

                    if b == SURE:
                        held = pool.value_load(counts_held[0:1, bass.ds(2 * k + u, 1)], min_val=0, max_val=NTOK)
                    for i in range(UT):
                        if b < SURE or i == 0:
                            scatter(i)
                        else:
                            with pool.If(held > P * (UT * b + i)):
                                scatter(i)
                    if b > SURE:
                        landed(b - 1)
                    elif b == 0 and not (isinstance(k, int) and k == 0 and local == 0):
                        landed(NU - 1)

            each_pair(pool, pair)
            landed(NU - 1)

        @block.scalar
        def _(act):
            act.preload_act_table_set("natural_log_exp_and_others")

            def square_ahead(G):
                act.wait_ge(x_centred, G.g + 1)
                wait_past(act, squares_summed[0], G.g)
                nc.scalar.activation(sq1[:].rearrange("p s c -> p (s c)"), psC[:], ACT.Square).then_inc(squared1, 1)

            def rough_root(G, norm):
                act.wait_ge(squares_summed[norm], G.g + 1)
                nc.scalar.activation(logvar[norm][:], squares[norm][:], ACT.Ln, bias=eps[norm][:, 0:1],
                                     scale=1.0 / C).then_inc(log_done[norm], 1)
                act.wait_ge(log_done[norm], G.g + 1)
                nc.scalar.activation(root[norm][:], logvar[norm][:], ACT.Exp, scale=-0.5).then_inc(root_done[norm], 1)

            def a_turn(T):
                i = T.i
                if T.front:
                    act.wait_ge(col_mm, i + 1)
                    nc.scalar.copy(col[:], p_col).then_inc(col_done, 1)
                if T.back:
                    rough_root(T.back, 1)
                if T.front:
                    act.wait_ge(freq_mm, i + 1)
                    nc.scalar.copy(row_freq[:], p_freq).then_inc(freq_done, 1)
                    nc.scalar.activation(cf_exp[:], p_z, ACT.Exp, bias=ncb[:, 0:1], scale=-1.0).then_inc(cf_exp_done, 1)
                    act.wait_ge(cf_col_done, i + 1)
                    nc.scalar.copy(colb[:], cf_col[:].unsqueeze(2).to_broadcast([C, 2, P])).then_inc(colb_done, 1)
                if T.back:
                    act.wait_ge(below_done, i)
                    nc.scalar.activation(expo[:], below[:], ACT.Exp).then_inc(exp_done, 1)
                if T.ahead:
                    square_ahead(T.ahead)
                for half in range(2):
                    if T.front:
                        act.wait_ge(x1_turned, 2 * i + half + 1)
                        nc.scalar.copy(x1T[:, 512 * half:512 * (half + 1)], psT[:]).then_inc(x1T_done, 1)
                    if T.ahead and half == 0:
                        rough_root(T.ahead, 0)
                if T.front:
                    nc.scalar.copy(x1_all[:, bass.ds(i, 1), :].rearrange("p a n -> p (a n)"),
                                   x1[:].rearrange("p s c -> p (s c)")).then_inc(x1_kept, 1)
                    for half in range(2):
                        act.wait_ge(x1_centred, 2 * i + half + 1)
                        wait_past(act, squares_summed[1], i)
                        nc.scalar.activation(sq2[:, 8 * half:8 * half + 8, :].rearrange("p s c -> p (s c)"),
                                             psD[:, 512 * half:512 * (half + 1)], ACT.Square).then_inc(squared2, 1)

            act.wait_ge(eps_set, 2)
            square_ahead(Group(0, 0))
            rough_root(Group(0, 0), 0)
            act.wait_ge(setup_mm, N_SETUP)
            nc.scalar.copy(cgw[:], psM[:, 0:2 * E]).then_inc(setup_done, 1)
            nc.scalar.copy(cwT[:], psM[0:C, 64:64 + C]).then_inc(setup_done, 1)
            nc.scalar.mul(ncb[:], psM[0:C, 128:129], -1.0).then_inc(setup_done, 1)
            nc.scalar.copy(b1_cols[:], psM[:, 256:256 + 2 * E]).then_inc(setup_done, 1)
            each_turn(act, a_turn)

            act.wait_ge(big_in, N_BIG)
            w1p = wp_all[:].rearrange("p e (a f) -> p e a f", a=3)
            nc.scalar.copy(w1p[:, :, 0, :], w1_all[:])
            nc.scalar.copy(w1p[C:P, :, 2, :], w1_all[C:P, :, :]).then_inc(parts_done, 1)
            act.wait_ge(parts_left, 1)
            nc.scalar.copy(w1p[:, :, 1, :], w1_all[:]).then_inc(parts_done, 1)

            def split_slots(k, u, part, cols=slice(0, ST)):
                if part == 1:
                    if cols.stop == UT:
                        act.wait_ge(first_slots, 16)
                    else:
                        act.wait_ge(slot_loaded[u], 16 * (k + 1))
                    wait_past(act, slots_turned, (2 * k + u - 1) * NU)
                    nc.scalar.copy(x_split[u][:, cols, 1, :], slot_in[u][:, cols, 0:C]).then_inc(x_part1, 1)
                else:
                    act.wait_ge(x_left, pieces(k, u, cols))
                    nc.scalar.copy(x_split[u][:, cols, 0, :], x_rest[:, cols, :]).then_inc(x_part2, 1)

            def take_turned(k, local):
                k, local, n, e, u, j, w = unit_at(k, local)
                act.wait_ge(slots_turned, n + 1)
                wait_past(act, hid_mm, n - 1)
                nc.scalar.copy(xT[w][:].rearrange("p a n -> p (a n)"), psTb).then_inc(xT_done, 1)

            def relu(k, local):
                k, local, n, e, u, j, w = unit_at(k, local)
                if j == 0:
                    act.wait_ge(b1_done, e + 1)
                act.wait_ge(hid_mm, n + 1)
                wait_past(act, y_mm, n - 1)
                for half in range(2):
                    last = nc.scalar.activation(hid[w][:, half, :], (psX, psC)[w][:, 512 * half:512 * (half + 1)],
                                                ACT.Relu, bias=b1_in[u][:, half:half + 1])
                last.then_inc(hid_done, 1)

            for part in (1, 2):
                split_slots(0, 0, part, FIRST)
            take_turned(0, 0)
            split_slots(0, 0, 1, OTHERS)
            relu(0, 0)
            split_slots(0, 0, 2, OTHERS)
            take_turned(0, 1)

            def pair(k, last):
                for local in range(2 * NU):
                    if not last or local + 2 < 2 * NU:
                        take_turned(k, local + 2)
                    if not last or local + 1 < 2 * NU:
                        relu(k, local + 1)
                    nk, nu = (k, 1) if local < NU else (k + 1, 0)
                    if local % NU in SPLIT_AT and not (last and local >= NU):
                        split_slots(nk, nu, 1 + SPLIT_AT.index(local % NU))

            each_pair(act, pair)

            def take_out(g, k, b):
                act.wait_ge(out_turned, g + 1)
                wait_past(act, stored[b], k * 16)
                nc.scalar.copy(o_sb[b].rearrange("q (p t) -> q t p", t=TT),
                               (psX, psC)[b % 2][:].rearrange("q (t p) -> q t p", t=TT)).then_inc(out_copied, 1)
                act.wait_ge(out_copied, g + 1)
                act.dma_start(out_rows[bass.ds(g * P, P), :], o_sb[b]).then_inc(stored[b], 16)

            each_out(act, take_out)

        @block.vector
        def _(dve):
            nc.vector.memset(gw[:], 0.0).then_inc(gw_zero, 1)
            for norm, value in enumerate((1e-6, 1e-5)):
                nc.vector.memset(eps[norm][:], value).then_inc(eps_set, 1)
            nc.vector.memset(zero_row[:], 0.0).then_inc(empty_set, 1)
            nc.vector.memset(empty_row[:], 1.0).then_inc(empty_set, 1)
            nc.vector.memset(carry[:], 0.0).then_inc(dve_step, 1)
            dve.wait_ge(weights_in, N_WEIGHTS)
            nc.vector.tensor_copy(gb[:], gb8[:].unsqueeze(1).unsqueeze(3)
                                  .to_broadcast([P, 2, E, TT])).then_inc(dve_step, 1)
            dve.wait_ge(const_in, N_CONST)
            nc.vector.tensor_copy(token_f[:], token_of).then_inc(dve_step, 1)
            nc.vector.tensor_copy(ident_b[:], ident).then_inc(ident_ready, 1)
            dve.wait_ge(dve_step, SET_STEPS - 1)

            class Steps:

                def __init__(self, base):
                    self.base, self.n = base, 0

                def done(self, instruction):
                    instruction.then_inc(dve_step, 1)
                    self.n += 1
                    return self.n

                def wait(self, n):
                    dve.wait_ge(dve_step, self.base + n)

            def sum_squares(st, i, norm, eps_value):
                nc.vector.tensor_reduce(squares[norm][:], (sq1, sq2)[norm][:], AX.X, ALU.add).then_inc(
                    squares_summed[norm], 1)
                dve.wait_ge(squares_summed[norm], i + 1)
                return st.done(nc.vector.tensor_scalar(variance[norm][:], squares[norm][:], 1.0 / C, eps_value,
                                                       ALU.mult, ALU.add))

            def newton_step(st, i, norm):
                y, q = root[norm][:], newton[norm][:]
                dve.wait_ge(root_done[norm], i + 1)
                st.wait(st.done(nc.vector.tensor_tensor(q, y, y, ALU.mult)))
                st.wait(st.done(nc.vector.scalar_tensor_tensor(q, q, -0.5, variance[norm][:], ALU.mult, ALU.mult)))
                st.wait(st.done(nc.vector.scalar_tensor_tensor(rstd[norm][:], q, 1.5, y, ALU.add, ALU.mult)))

            def over_c(tile):
                return tile.unsqueeze(2).to_broadcast([P, S, C])

            def thc(tile):
                return tile.rearrange("p (t h) c -> p t h c", h=2)

            def ht_e(tile):
                return tile[:].rearrange("p h e t -> p h t e")

            def th(tile):
                return tile[:].rearrange("p (t h) -> p h t", h=2)

            def over_e(tile):
                return th(tile).unsqueeze(2).to_broadcast([P, 2, E, TT])

            def a_turn(T):
                if isinstance(T.i, int) and T.i == 0:
                    st = Steps(SET_STEPS)
                else:
                    st = Steps(SET_STEPS + FIRST_STEPS + TURN_STEPS * (T.i - 1) - (0 if T.front else 1))
                i = T.i
                if T.front:
                    newton_step(st, i, 0)
                    nc.vector.tensor_tensor(xn[:], psC[:].rearrange("p (s c) -> p s c", c=C), over_c(rstd[0][:]),
                                            ALU.mult).then_inc(xn_done, 1)
                    dve.wait_ge(xn_done, i + 1)
                    nc.vector.tensor_reduce(mean_n[:], xn[:], AX.X, ALU.add).then_inc(mean_done, 1)
                    dve.wait_ge(mean_done, i + 1)
                    nc.vector.tensor_tensor(mean_q[:], mean_n[:].unsqueeze(1).to_broadcast([P, 4, S]),
                                            own_q.unsqueeze(2).to_broadcast([P, 4, S]),
                                            ALU.mult).then_inc(mean_split, 1)
                if T.back:
                    dve.wait_ge(squared2, 2 * i)
                    sum_squares(st, i - 1, 1, 1e-5)
                    u = T.back.u
                    newton_step(st, i - 1, 1)
                    wait_past(dve, rows_out[u], T.back.half * S * 16)
                    nc.vector.tensor_tensor(rows[u][:, :, 0:C], psD[:].rearrange("p (s c) -> p s c", c=C),
                                            over_c(rstd[1][:]), ALU.mult).then_inc(rows_done, 1)
                    dve.wait_ge(logits_mm, i)
                    nc.vector.tensor_tensor(
                        lg[:].rearrange("p h e t -> p t h e"), p_log.rearrange("p (t h e) -> p t h e", t=TT, h=2),
                        rstd[1][:].rearrange("p (t h) -> p t h", h=2).unsqueeze(3).to_broadcast([P, TT, 2, E]),
                        ALU.mult).then_inc(logits_read, 1)
                    nc.vector.tensor_copy(rows[u][:].bitcast(u32)[:, :, C + 1], token_f[:]).then_inc(numbered, 1)
                    dve.wait_ge(logits_read, i)
                    st.wait(st.done(nc.vector.tensor_tensor(lgb[:], lg[:], gb[:], ALU.add)))
                    st.wait(st.done(nc.vector.tensor_reduce(th(top), ht_e(lgb), AX.X, ALU.max)))
                    nc.vector.tensor_tensor(below[:], lgb[:], over_e(top), ALU.subtract).then_inc(below_done, 1)
                if T.front:
                    dve.wait_ge(cf_exp_done, i + 1)
                    st.wait(st.done(nc.vector.tensor_scalar(cf_den[:], cf_exp[:], 1.0, None, ALU.add)))
                    nc.vector.reciprocal(cf_col[:], cf_den[:]).then_inc(cf_col_done, 1)
                if T.back:
                    dve.wait_ge(numbered, i)
                    st.done(nc.vector.tensor_scalar(token_f[:], token_f[:], float(S * P), None, ALU.add))
                    dve.wait_ge(below_done, i)
                    st.wait(st.done(nc.vector.scalar_tensor_tensor(
                        cand[:].rearrange("p h e t -> p (h e t)"), below[:].rearrange("p h e t -> p (h e t)"), 0.0,
                        e_less_8, ALU.is_equal, ALU.mult)))
                    st.wait(st.done(nc.vector.tensor_reduce(th(pick), ht_e(cand), AX.X, ALU.min)))
                    st.wait(st.done(nc.vector.tensor_tensor(hot[:], cand[:], over_e(pick), ALU.is_equal)))
                    nc.vector.tensor_tensor_scan(run[:].rearrange("p h e t -> p (h e t)"), scan_keep,
                                                 hot[:].rearrange("p h e t -> p (h e t)"), 0.0,
                                                 ALU.mult, ALU.add).then_inc(run_done, 1)
                    dve.wait_ge(exp_done, i)
                    st.wait(st.done(nc.vector.tensor_reduce(th(den), ht_e(expo), AX.X, ALU.add)))
                    st.done(nc.vector.reciprocal(rows[u][:, :, C], den[:]))
                if T.front:
                    dve.wait_ge(sf_mm, i + 1)
                    nc.vector.tensor_tensor(
                        sf_all[:], p_sf.rearrange("p (h q t) -> p h q t", h=2, q=4),
                        own_q.unsqueeze(1).unsqueeze(3).to_broadcast([P, 2, 4, TT]), ALU.mult).then_inc(sf_read, 1)
                    dve.wait_ge(sf_read, i + 1)
                    st.wait(st.done(nc.vector.tensor_reduce(th(sf), sf_all[:].rearrange("p h q t -> p h t q"),
                                                            AX.X, ALU.add)))
                    dve.wait_ge(cf_mm, i + 1)
                    nc.vector.tensor_tensor(
                        thc(mix[:]), p_cf.rearrange("p (h c) -> p h c", h=2).unsqueeze(1).to_broadcast([P, TT, 2, C]),
                        thc(over_c(sf[:])), ALU.add).then_inc(cf_read, 1)
                    dve.wait_ge(cf_read, i + 1)
                    st.wait(st.done(nc.vector.tensor_tensor(mix[:], mix[:], xn[:], ALU.mult)))
                    dve.wait_ge(x_turned, i + 1)
                    wait_past(dve, x1_kept, i)
                    nc.vector.tensor_tensor(x1[:], mix[:], psX[:].rearrange("p (s c) -> p s c", c=C),
                                            ALU.add).then_inc(x1_done, 1)
                if T.ahead:
                    dve.wait_ge(squared1, i + 2)
                    sum_squares(st, i + 1, 0, 1e-6)
                if T.back:
                    dve.wait_ge(base_mm, i)
                    st.wait(st.done(nc.vector.tensor_tensor(
                        start[:], p_base.rearrange("p (h e) -> p h e", h=2),
                        carry[:].unsqueeze(1).to_broadcast([P, 2, E]), ALU.add)))
                    nc.vector.tensor_tensor(carry[:], carry[:], p_sum, ALU.add).then_inc(base_read, 1)
                    st.wait(st.done(nc.vector.tensor_tensor(
                        place[:], run[:], start[:].unsqueeze(3).to_broadcast([P, 2, E, TT]), ALU.add)))
                    st.wait(st.done(nc.vector.tensor_tensor(own[:], place[:], hot[:], ALU.mult)))
                    st.wait(st.done(nc.vector.tensor_reduce(th(rank), ht_e(own), AX.X, ALU.add)))
                    st.done(nc.vector.scalar_tensor_tensor(slot_f[:], pick[:], float(CAP), rank[:], ALU.mult, ALU.add))
                    st.wait(st.done(nc.vector.tensor_scalar(over[:], rank[:], float(CAP), float(1 << 20),
                                                            ALU.is_gt, ALU.mult)))
                    nc.vector.scalar_tensor_tensor(slots[u][:], slot_f[:], float(E * CAP - 1), over[:], ALU.add,
                                                   ALU.add).then_inc(slots_done, 1)
                assert st.n == (FIRST_STEPS if not T.back else LAST_STEPS if not T.front else
                                TURN_STEPS if T.ahead else TURN_STEPS - 1)

            st = Steps(SET_STEPS - 1)
            dve.wait_ge(squared1, 1)
            st.wait(sum_squares(st, 0, 0, 1e-6))
            each_turn(dve, a_turn)

            nc.vector.tensor_copy(counts_held[:], carry[:]).then_inc(counts_ready, 1)
            w1p = wp_all[:].rearrange("p e (a f) -> p e a f", a=3)
            dve.wait_ge(parts_done, 1)
            nc.vector.tensor_tensor(w1_all[:], w1_all[:], w1p[:, :, 0, :], ALU.subtract).then_inc(parts_left, 1)
            dve.wait_ge(parts_left, 1)
            dve.wait_ge(parts_done, 2)
            nc.vector.tensor_tensor(w1p[0:C, :, 2, :], w1_all[0:C, :, :], w1p[0:C, :, 1, :],
                                    ALU.subtract).then_inc(parts_left, 1)
            dve.wait_ge(b2_in, 16)

            def split_slots(k, u, part, cols=slice(0, ST)):
                if part == 1:
                    dve.wait_ge(x_part1, pieces(k, u, cols))
                    wait_past(dve, x_part3, pieces(k, u, cols) - 1)
                    nc.vector.tensor_tensor(x_rest[:, cols, :], slot_in[u][:, cols, 0:C], x_split[u][:, cols, 1, :],
                                            ALU.subtract).then_inc(x_left, 1)
                else:
                    dve.wait_ge(x_part2, pieces(k, u, cols))
                    nc.vector.tensor_tensor(x_split[u][:, cols, 2, :], x_rest[:, cols, :], x_split[u][:, cols, 0, :],
                                            ALU.subtract).then_inc(x_part3, 1)

            def note(k, u):
                e = 2 * k + u
                dve.wait_ge(slot_loaded[u], 16 * (k + 1))
                for b in range(SURE):
                    wait_past(dve, y_out[b], (e - 1) * UT * 16)
                wait_past(dve, y_free, (e - 1) * (NU - SURE))
                nc.vector.tensor_copy(meta[u][:], slot_in[u][:, :, C:C + 2]).then_inc(meta_done, 1)

            def bias_ahead(k, u):
                nc.vector.tensor_copy(b1_in[u][:], b1_cols[:, bass.ds((2 * k + u) * 2, 2)]).then_inc(b1_done, 1)

            def scaled(k, local, st):
                k, local, n, e, u, j, w = unit_at(k, local)
                b = local % NU
                y = ys[b]
                dve.wait_ge(y_mm, n + 1)
                dve.wait_ge(meta_done, e + 1)
                if b < SURE:
                    wait_past(dve, y_out[b], e * UT * 16)
                else:
                    wait_past(dve, y_free, (e - 1) * (NU - SURE) + b - SURE + 1)
                nc.vector.tensor_tensor(
                    with_b2[:], psD[:, 512 * w:512 * w + UT * C].rearrange("p (i c) -> p i c", c=C),
                    b2_all[:, bass.ds(e, 1), :].to_broadcast([P, UT, C]), ALU.add).then_inc(y_read, 1)
                dve.wait_ge(y_read, n + 1)
                st.wait(st.done(nc.vector.tensor_tensor(
                    y[:], with_b2[:], meta[u][:, UT * j:UT * (j + 1), 0:1].to_broadcast([P, UT, C]), ALU.mult)))

            def guard(k, local, st):
                k, local, n, e, u, j, w = unit_at(k, local)
                y = ys[local % NU]
                nc.vector.tensor_scalar(bad[:], y[:], 0.0, 0.0, ALU.mult, ALU.not_equal)
                nc.vector.tensor_scalar(neg[:], y[:], 0.0, -1e4, ALU.is_lt, ALU.mult)
                st.wait(st.done(nc.vector.tensor_scalar(pos[:], y[:], 0.0, 1e4, ALU.is_gt, ALU.mult)))
                st.wait(st.done(nc.vector.tensor_tensor(edge[:], neg[:], pos[:], ALU.add)))

            def replace(k, local):
                k, local, n, e, u, j, w = unit_at(k, local)
                flat = "p i c -> p (i c)"
                nc.vector.copy_predicated(ys[local % NU][:].rearrange(flat), bad[:].bitcast(u32).rearrange(flat),
                                          edge[:].rearrange(flat)).then_inc(y_done, 1)

            bias_ahead(0, 0)
            for cols in (FIRST, OTHERS):
                for part in (1, 2):
                    split_slots(0, 0, part, cols)
            note(0, 0)

            def pair(k, last):
                for local in range(2 * NU):
                    st = Steps(A_STEPS + 3 * (2 * NU * k + local))
                    nk, nu = (k, 1) if local < NU else (k + 1, 0)
                    ahead = not (last and local >= NU)
                    splits = ahead and local % NU in SPLIT_AT
                    hurry = isinstance(k, int) and k == 0 and local < NU
                    if splits and not hurry:
                        split_slots(nk, nu, 1 + SPLIT_AT.index(local % NU))
                    scaled(k, local, st)
                    guard(k, local, st)
                    nc.vector.memset(edge_free[:], 0.0)
                    replace(k, local)
                    if splits and hurry:
                        split_slots(nk, nu, 1 + SPLIT_AT.index(local % NU))
                    if ahead and local % NU == 1:
                        bias_ahead(nk, nu)
                    if ahead and local % NU == NU - 1:
                        note(nk, nu)

            each_pair(dve, pair)

            def add_output(g, k, b):
                dve.wait_ge(y_loaded[b], 16 * (k + 1))
                wait_past(dve, out_turned, g - 1)
                nc.vector.tensor_tensor(
                    total[b % 2][:].rearrange("p (t h) c -> p h t c", h=2),
                    x1_all[:, bass.ds(g, 1), :].rearrange("p a (t h c) -> p (a h) t c", t=TT, h=2),
                    y_in[b], ALU.add).then_inc(total_done, 1)

            each_out(dve, add_output)

        @block.tensor
        def _(pe):
            def pixels(G):
                return x_in[G.u][:].rearrange("q (p t) -> q t p", t=TT)

            def keep_busy(bank, times):
                for _ in range(times):
                    nc.tensor.matmul(bank[:, 0:4 * P], ident_b[:], ident_b[:].unsqueeze(1).to_broadcast([P, 4, P]),
                                     start=True, stop=True)

            def centre_ahead(G, half):
                if half == 0:
                    pe.wait_ge(x_loaded[G.u], 16 * (G.half + 1))
                    wait_past(pe, xn_done, G.g)
                for t in range(half * TT // 2, (half + 1) * TT // 2):
                    last = nc.tensor.matmul(psC[:, t * P:(t + 1) * P], pixels(G)[:, t, :], centre,
                                            start=True, stop=True)
                if half == 1:
                    last.then_inc(x_centred, 1)

            def a_turn(T):
                i = T.i
                if T.front:
                    pe.wait_ge(xn_done, i + 1)
                    wait_past(pe, x1T_done, 2 * i)
                    for h in range(2):
                        last = nc.tensor.matmul(p_col[:, h:h + 1], xn[0:1, h, :], ones[0:1, 0:1], start=True, stop=True)
                    last.then_inc(col_mm, 1)
                if T.back:
                    pe.wait_ge(sf_read, i)
                    for t in range(TT):
                        last = nc.tensor.matmul(p_log[:, t * 2 * E:(t + 1) * 2 * E], x1T[:, t * P:(t + 1) * P], cgw[:],
                                                start=True, stop=True)
                    last.then_inc(logits_mm, 1)
                if T.ahead:
                    centre_ahead(T.ahead, 0)
                if T.front:
                    pe.wait_ge(mean_split, i + 1)
                    pe.wait_ge(col_done, i + 1)
                    nc.tensor.matmul(p_freq, mean_q[:].rearrange("p q s -> p (q s)"), dft_rows, start=True, stop=True)
                    nc.tensor.matmul(p_z, cwT[:], col[:], start=True, stop=True).then_inc(freq_mm, 1)
                if T.ahead:
                    centre_ahead(T.ahead, 1)
                if T.front:
                    wait_past(pe, x1_done, i)
                    for t in range(TT):
                        last = nc.tensor.transpose(psX[:, t * P:(t + 1) * P], pixels(T.front)[:, t, :], ident)
                    last.then_inc(x_turned, 1)
                    pe.wait_ge(freq_done, i + 1)
                    wait_past(pe, logits_read, i)
                    for a in range(2):
                        last = nc.tensor.matmul(p_sf, row_freq[:, a * P:(a + 1) * P], dft_cols[:, a, :],
                                                start=(a == 0), stop=(a == 1))
                    last.then_inc(sf_mm, 1)
                    pe.wait_ge(colb_done, i + 1)
                    for h in range(2):
                        last = nc.tensor.matmul(p_cf[:, h * C:(h + 1) * C], colb[:, h, :], ident[0:C, 0:C],
                                                start=True, stop=True)
                    last.then_inc(cf_mm, 1)
                if T.back:
                    pe.wait_ge(run_done, i)
                    pe.wait_ge(rows_done, i)
                    counts = run[:].rearrange("p h e t -> p (h e) t")[:, :, TT - 1]
                    nc.tensor.matmul(p_base[:, 0:E], before, counts[:, 0:E], start=True, stop=True)
                    nc.tensor.matmul(p_base[:, E:], before, counts[:, E:], start=True, stop=False)
                    nc.tensor.matmul(p_base[:, E:], ones, counts[:, 0:E], start=False, stop=True)
                    nc.tensor.matmul(p_sum, ones, counts[:, 0:E], start=True, stop=False)
                    nc.tensor.matmul(p_sum, ones, counts[:, E:], start=False, stop=True).then_inc(base_mm, 1)
                if T.front:
                    pe.wait_ge(sf_read, i + 1)
                    keep_busy(psM, 12)
                    pe.wait_ge(x1_done, i + 1)

                    def turn_half(half):
                        for a in range(TT // 2):
                            t = half * TT // 2 + a
                            last = nc.tensor.transpose(psT[:, a * P:(a + 1) * P],
                                                       x1[:, 2 * t:2 * t + 2, :].rearrange("p s c -> p (s c)"), ident)
                        last.then_inc(x1_turned, 1)

                    def centre_half(half):
                        for t in range(half * TT // 2, (half + 1) * TT // 2):
                            last = nc.tensor.matmul(psD[:, t * P:(t + 1) * P], x1T[:, t * P:(t + 1) * P], centre,
                                                    start=True, stop=True)
                        last.then_inc(x1_centred, 1)

                    turn_half(0)
                    pe.wait_ge(x1T_done, 2 * i + 1)
                    turn_half(1)
                    centre_half(0)
                    wait_past(pe, base_read, i)
                    pe.wait_ge(x1T_done, 2 * i + 2)
                    centre_half(1)

            pe.wait_ge(centre_in, 16)
            for half in range(2):
                centre_ahead(Group(0, 0), half)
            pe.wait_ge(const_in, N_CONST)
            pe.wait_ge(weights_in, N_WEIGHTS)
            nc.tensor.matmul(psM[:, 0:2 * E], centre, gw[:], start=True, stop=True).then_inc(setup_mm, 1)
            nc.tensor.transpose(psM[0:C, 64:64 + C], cw[:], ident[0:C, 0:C]).then_inc(setup_mm, 1)
            nc.tensor.matmul(psM[0:C, 128:129], cb[:], ones[0:1, 0:1], start=True, stop=True).then_inc(setup_mm, 1)
            nc.tensor.transpose(psM[:, 256:256 + 2 * E], b1_rows[:], ident[0:2 * E, 0:2 * E]).then_inc(setup_mm, 1)
            pe.wait_ge(setup_done, N_SETUP)
            pe.wait_ge(ident_ready, 1)
            each_turn(pe, a_turn)

            def turn(k, local):
                k, local, n, e, u, j, w = unit_at(k, local)
                if isinstance(n, int) and n == 0:
                    pe.wait_ge(x_part3, 1)
                elif isinstance(n, int) and n == 1:
                    pe.wait_ge(x_part3, 2)
                elif j == 0:
                    pe.wait_ge(x_part3, e + 2)
                wait_past(pe, xT_done, n)
                for kind in range(2):
                    for i in range(UT):
                        at = 512 * kind + P * i
                        last = nc.tensor.transpose(psTb[:, at:at + P],
                                                   x_split[u][:, UT * j + i, kind:kind + 2, :]
                                                   .rearrange("p a c -> p (a c)"), ident_b[:])
                last.then_inc(slots_turned, 1)

            def up(k, local):
                k, local, n, e, u, j, w = unit_at(k, local)
                if j == 0:
                    pe.wait_ge(w_loaded[u], 32 * (k + 1))
                pe.wait_ge(xT_done, n + 1)
                wait_past(pe, hid_done, n - 1)
                for half in range(2):
                    for part in range(3):
                        at = F * part + P * half
                        last = nc.tensor.matmul((psX, psC)[w][:, 512 * half:512 * (half + 1)], wp[u][:, at:at + P],
                                                xT[w][:, part // 2, :], start=(part == 0), stop=(part == 2))
                last.then_inc(hid_mm, 1)

            def down(k, local):
                k, local, n, e, u, j, w = unit_at(k, local)
                pe.wait_ge(hid_done, n + 1)
                wait_past(pe, y_read, n - 1)
                for i in range(UT):
                    o = psD[:, 512 * w + C * i:512 * w + C * (i + 1)]
                    for half in range(2):
                        last = nc.tensor.matmul(o, hid[w][:, half, P * i:P * (i + 1)], w2_in[u][:, half, :],
                                                start=(half == 0), stop=(half == 1))
                last.then_inc(y_mm, 1)

            pe.wait_ge(all_sent, 1)
            keep_busy(psX, 18)
            turn(0, 0)
            keep_busy(psC, 4)
            up(0, 0)
            keep_busy(psC, 5)
            down(0, 0)
            turn(0, 1)
            keep_busy(psC, 4)
            turn(0, 2)
            up(0, 1)
            keep_busy(psX, 5)

            def pair(k, last):
                for local in range(2 * NU):
                    early = isinstance(k, int) and k == 0 and local < 2
                    if early:
                        if local:
                            down(k, local)
                    if not (isinstance(k, int) and k == 0 and local == 0):
                        if not last or local + 2 < 2 * NU:
                            turn(k, local + 2)
                        if not last or local + 1 < 2 * NU:
                            up(k, local + 1)
                    if not early:
                        down(k, local)

            each_pair(pe, pair)

            def turn_output(g, k, b):
                pe.wait_ge(total_done, g + 1)
                wait_past(pe, out_copied, g - 1)
                for t in range(TT):
                    last = nc.tensor.transpose((psX, psC)[b % 2][:, t * P:(t + 1) * P],
                                               total[b % 2][:, 2 * t:2 * t + 2, :].rearrange("p s c -> p (s c)"), ident)
                last.then_inc(out_turned, 1)

            each_out(pe, turn_output)


_INS = ["x", "L0_conv_W", "L0_conv_b", "L0_ffn_gate_w", "L0_ffn_gate_b", "L0_ffn_w1", "L0_ffn_b1", "L0_ffn_w2",
        "L0_ffn_b2"]


def constants():
    import numpy as np

    p = np.arange(P)
    ident = np.eye(P)
    same_half = (p[:, None] // C == p[None, :] // C)
    centre = ident - same_half / C
    before = (p[:, None] < p[None, :]).astype(float)
    ones = np.ones((P, P))
    i, q = p // 4, p % 4
    turns = 2 * np.pi / SIDE
    angle = turns * np.outer(i, i)
    rows = np.stack([np.cos(angle), np.sin(angle)], 1) / C
    own_q = (q[:, None] == np.arange(4)[None, :]).astype(float)
    keep = np.broadcast_to(np.arange(TT) != 0, (2 * E, TT)).reshape(1, -1).repeat(P, 0).astype(float)
    e_less_8 = np.broadcast_to((np.arange(E) - E)[None, :, None], (2, E, TT)).reshape(1, -1).repeat(P, 0)
    t, h = np.arange(S) // 2, np.arange(S) % 2
    token = TT * p[:, None] + t[None, :] + HW * h[None, :]
    const = np.concatenate([ident, centre, before, ones, rows.reshape(P, -1), own_q, keep, e_less_8, token], 1)
    cols = np.zeros((4, S, 2, 2, SIDE))
    for s in range(S):
        for r in range(4):
            angle = turns * (TT * r + t[s]) * np.arange(SIDE)
            cols[r, s, 0, h[s], :] = np.cos(angle)
            cols[r, s, 1, h[s], :] = -np.sin(angle)
    return const.astype(np.float32), cols.reshape(4 * S, -1).astype(np.float32)


def kernel(**inputs):
    import numpy as _np
    import concourse.bacc as _bacc
    from concourse import mybir as _mybir
    from concourse.bass_utils import run_bass_kernel_spmd as _run

    nc = _bacc.Bacc("TRN2", target_bir_lowering=False, num_devices=1)
    arrays, args = {}, []
    const, dft = constants()
    for name, a in [(n, inputs[n]) for n in _INS] + [("const", const), ("dft", dft)]:
        a = _np.ascontiguousarray(a)
        arrays[f"in_{name}_dram"] = a
        args.append(nc.dram_tensor(f"in_{name}_dram", a.shape, _mybir.dt.from_np(a.dtype), kind="ExternalInput").ap())
    args.append(nc.dram_tensor("out_dram", (NB, C, 32, 32), _mybir.dt.float32, kind="ExternalOutput").ap())
    build(nc, *args)
    r = _run(nc, [arrays], core_ids=[0])
    return r.results[0]["out_dram"]
```
